# Optimizing a Trainium2 kernel written in Bass

```python
import numpy as np
import jax
import jax.numpy as jnp

def _softmax(x, axis=-1):
    return jax.nn.softmax(x, axis=axis)

def _gelu(x):
    return jax.nn.gelu(x, approximate=True)

def _silu(x):
    return jax.nn.silu(x)

def _sigmoid(x):
    return jax.nn.sigmoid(x)

def _layernorm(x, axis=-1, eps=1e-05):
    m = jnp.mean(x, axis=axis, keepdims=True)
    v = jnp.var(x, axis=axis, keepdims=True)
    return (x - m) / jnp.sqrt(v + eps)

def _scatter_add(tgt, idx, src, axis=0):
    return tgt.at[idx].add(src)

def _segment_sum(src, seg, n):
    return jax.ops.segment_sum(src, seg, n)
kernel_name = 'mk_prb_d1_jaxref_r8_8c5140'

def setup_inputs(seed: int=0):
    np.random.seed(seed)
    _w = jnp.asarray

    def _L0_attn_setup():
        import jax, jax.numpy as jnp
        import numpy as np
        import math
        D_MODEL = 128
        N_HEADS = 16
        D_HEAD = D_MODEL // N_HEADS
        WINDOW = 32

        def _attention(x, Wq, bq, Wk, bk, Wv, bv, Wo, bo):
            B, T, C = x.shape
            W = min(WINDOW, T)
            scale = math.sqrt(D_HEAD)

            def proj(Wm, bm):
                return (x @ Wm.T + bm).reshape(B, T, N_HEADS, D_HEAD).transpose(0, 2, 1, 3)
            Q, K, V = (proj(Wq, bq), proj(Wk, bk), proj(Wv, bv))
            scores = jnp.einsum('bhqd,bhkd->bhqk', Q, K) / scale
            idx = jnp.arange(T)
            row = idx[:, None]
            col = idx[None, :]
            allowed = (col <= row) & (row - col < W)
            scores = jnp.where(allowed[None, None], scores, -jnp.inf)
            attn = jax.nn.softmax(scores, axis=-1)
            attn = jnp.nan_to_num(attn, nan=0.0)
            out = jnp.einsum('bhqk,bhkd->bhqd', attn, V)
            out = out.transpose(0, 2, 1, 3).reshape(B, T, C)
            return out @ Wo.T + bo
        key = jax.random.key(seed)
        ks = jax.random.split(key, 9)
        B, T = (2, 256)
        x = jax.random.normal(ks[0], (B, T, D_MODEL), dtype=jnp.float32)
        s = 1.0 / math.sqrt(D_MODEL)
        Wq = jax.random.uniform(ks[1], (D_MODEL, D_MODEL), jnp.float32, -s, s)
        bq = jax.random.uniform(ks[2], (D_MODEL,), jnp.float32, -s, s)
        Wk = jax.random.uniform(ks[3], (D_MODEL, D_MODEL), jnp.float32, -s, s)
        bk = jax.random.uniform(ks[4], (D_MODEL,), jnp.float32, -s, s)
        Wv = jax.random.uniform(ks[5], (D_MODEL, D_MODEL), jnp.float32, -s, s)
        bv = jax.random.uniform(ks[6], (D_MODEL,), jnp.float32, -s, s)
        Wo = jax.random.uniform(ks[7], (D_MODEL, D_MODEL), jnp.float32, -s, s)
        bo = jax.random.uniform(ks[8], (D_MODEL,), jnp.float32, -s, s)
        return {'x': x, 'Wq': Wq, 'bq': bq, 'Wk': Wk, 'bk': bk, 'Wv': Wv, 'bv': bv, 'Wo': Wo, 'bo': bo}
    _L0_attn_in = _L0_attn_setup()

    def _L0_ffn_setup():
        import jax, jax.numpy as jnp
        import numpy as np
        E = 16
        H = 128
        F = 256
        TOP_K = 1
        B, S = (2, 128)
        key = jax.random.key(seed)
        ks = jax.random.split(key, 7)
        s = 0.02
        return {'hidden_states': jax.random.normal(ks[0], (B, S, H), jnp.float32), 'w_router': jax.random.normal(ks[1], (E, H), jnp.float32) * s, 'gate_up_proj': jax.random.normal(ks[2], (E, H, 2 * F), jnp.float32) * s, 'down_proj': jax.random.normal(ks[3], (E, F, H), jnp.float32) * s, 'w_gate': jax.random.normal(ks[4], (F, H), jnp.float32) * s, 'w_up': jax.random.normal(ks[5], (F, H), jnp.float32) * s, 'w_down': jax.random.normal(ks[6], (H, F), jnp.float32) * s}
    _L0_ffn_in = _L0_ffn_setup()
    _d = {'L0_attn_x': _L0_attn_in['x'], 'L0_attn_Wq': _L0_attn_in['Wq'], 'L0_attn_bq': _L0_attn_in['bq'], 'L0_attn_Wk': _L0_attn_in['Wk'], 'L0_attn_bk': _L0_attn_in['bk'], 'L0_attn_Wv': _L0_attn_in['Wv'], 'L0_attn_bv': _L0_attn_in['bv'], 'L0_attn_Wo': _L0_attn_in['Wo'], 'L0_attn_bo': _L0_attn_in['bo'], 'L0_ffn_w_router': _L0_ffn_in['w_router'], 'L0_ffn_gate_up_proj': _L0_ffn_in['gate_up_proj'], 'L0_ffn_down_proj': _L0_ffn_in['down_proj'], 'L0_ffn_w_gate': _L0_ffn_in['w_gate'], 'L0_ffn_w_up': _L0_ffn_in['w_up'], 'L0_ffn_w_down': _L0_ffn_in['w_down']}
    _x0 = _d['L0_attn_x']
    _d['L0_attn_x'] = jax.random.normal(jax.random.fold_in(jax.random.key(seed), 1), (32, 256, 128), dtype=_x0.dtype)
    del _x0
    return _d

def reference(L0_attn_x, L0_attn_Wq, L0_attn_bq, L0_attn_Wk, L0_attn_bk, L0_attn_Wv, L0_attn_bv, L0_attn_Wo, L0_attn_bo, L0_ffn_w_router, L0_ffn_gate_up_proj, L0_ffn_down_proj, L0_ffn_w_gate, L0_ffn_w_up, L0_ffn_w_down):

    def _L0_attn_ref(x, Wq, bq, Wk, bk, Wv, bv, Wo, bo):
        import jax, jax.numpy as jnp
        import numpy as np
        import math
        D_MODEL = 128
        N_HEADS = 16
        D_HEAD = D_MODEL // N_HEADS
        WINDOW = 32

        def _attention(x, Wq, bq, Wk, bk, Wv, bv, Wo, bo):
            B, T, C = x.shape
            W = min(WINDOW, T)
            scale = math.sqrt(D_HEAD)

            def proj(Wm, bm):
                return (x @ Wm.T + bm).reshape(B, T, N_HEADS, D_HEAD).transpose(0, 2, 1, 3)
            Q, K, V = (proj(Wq, bq), proj(Wk, bk), proj(Wv, bv))
            scores = jnp.einsum('bhqd,bhkd->bhqk', Q, K) / scale
            idx = jnp.arange(T)
            row = idx[:, None]
            col = idx[None, :]
            allowed = (col <= row) & (row - col < W)
            scores = jnp.where(allowed[None, None], scores, -jnp.inf)
            attn = jax.nn.softmax(scores, axis=-1)
            attn = jnp.nan_to_num(attn, nan=0.0)
            out = jnp.einsum('bhqk,bhkd->bhqd', attn, V)
            out = out.transpose(0, 2, 1, 3).reshape(B, T, C)
            return out @ Wo.T + bo
        return _attention(x, Wq, bq, Wk, bk, Wv, bv, Wo, bo)

    def _L0_ffn_ref(hidden_states, w_router, gate_up_proj, down_proj, w_gate, w_up, w_down):
        import jax, jax.numpy as jnp
        import numpy as np
        E = 16
        H = 128
        F = 256
        TOP_K = 1
        B, S = (2, 128)
        b, s, h = hidden_states.shape
        x = hidden_states.reshape(-1, h)
        logits = x @ w_router.T
        _, top_idx = jax.lax.top_k(logits, TOP_K)
        mask = jax.nn.one_hot(top_idx, E, dtype=logits.dtype).sum(axis=1)
        scores = jax.nn.sigmoid(logits) * mask
        masked_inputs = scores.T[:, :, None] * x[None, :, :]
        gate_up = jnp.einsum('eth,ehf->etf', masked_inputs, gate_up_proj)
        gate, up = jnp.split(gate_up, 2, axis=-1)
        expert_out = jnp.einsum('etf,efh->eth', up * jax.nn.silu(gate), down_proj)
        shared = jax.nn.silu(x @ w_gate.T) * (x @ w_up.T) @ w_down.T
        out = shared + expert_out.sum(axis=0)
        return out.reshape(b, s, h)
    x = L0_attn_x
    xn = _layernorm(x, axis=-1)
    x = x + _L0_attn_ref(xn, L0_attn_Wq, L0_attn_bq, L0_attn_Wk, L0_attn_bk, L0_attn_Wv, L0_attn_bv, L0_attn_Wo, L0_attn_bo) + _L0_ffn_ref(xn, L0_ffn_w_router, L0_ffn_gate_up_proj, L0_ffn_down_proj, L0_ffn_w_gate, L0_ffn_w_up, L0_ffn_w_down)
    return x

_drawn_inputs = setup_inputs


def setup_inputs(seed=0):
    import zlib

    import numpy as np

    out = dict(_drawn_inputs(seed))
    spreads = {}
    factors = {'L0_attn_bq': 64.0,
     'L0_attn_bk': 64.0,
     'L0_ffn_w_router': 8.0,
     'L0_ffn_gate_up_proj': 8.0,
     'L0_ffn_down_proj': 8.0,
     'L0_ffn_w_gate': 6.885,
     'L0_ffn_w_up': 6.822,
     'L0_ffn_w_down': 6.805,
     'L0_attn_Wq': 8.0,
     'L0_attn_Wk': 8.0,
     'L0_attn_Wv': 4.611,
     'L0_attn_bv': 8.0,
     'L0_attn_Wo': 4.23,
     'L0_attn_bo': 6.419}
    for name, (base, spread) in spreads.items():
        noise = np.random.default_rng([zlib.crc32(name.encode()), seed]).standard_normal(out[name].shape)
        drawn = base * np.exp(spread * noise) if base else spread * noise
        out[name] = jnp.asarray(drawn.astype(out[name].dtype))
    for name, factor in factors.items():
        out[name] = (out[name] * factor).astype(out[name].dtype)
    return out
```

```python
from contextlib import ExitStack

import concourse.bass as bass
import numpy as np
from concourse import mybir

F32, BF16 = mybir.dt.float32, mybir.dt.bfloat16
I32, U32, U16 = mybir.dt.int32, mybir.dt.uint32, mybir.dt.uint16
ALU = mybir.AluOpType
ACT = mybir.ActivationFunctionType
AX = mybir.AxisListType

P = 128
BATCHES, SEQ, D = 32, 256, 128
HEADS, DH, WINDOW = 16, 8, 32
EXPERTS, F = 16, 256
TOKENS = BATCHES * SEQ
TILES = TOKENS // P
PAIR = 2 * SEQ
PAIRS = TOKENS // PAIR
PT = PAIR // P
SORTED = TILES + EXPERTS
EPS = 1e-5
FAR = -float(2.0**100)
ROW = D + 4

PART_ROWS = [0, 8, 16, 64, 72, 80]
Q_PARTS = [0, 0, 1, 1, 0, 2]
K_PARTS = [0, 1, 0, 1, 2, 0]
FINE_ROWS = list(range(24, 64)) + list(range(88, 112))
BLOCK_ROWS = list(range(112, 120))
MAX_ROW = 120
ROWS_Q, ROWS_K = 120, 123

Q_ITEM = [(0, 0, 128), (128, 96, 160)]
K_ITEM = [(0, 0, 160), (128, 128, 128)]
ITEMS = 16
POST = {1: ("turn", 0), 3: ("turn", 1), 6: ("back", 0), 7: ("back", 1), 9: ("sum", 0), 10: ("sum", 1)}
EVEN = {11: ("gate", 0), 12: ("up", 0), 13: ("gate", 1), 14: ("up", 1)}
ODD = {11: ("q", 0), 12: ("k", 0), 13: ("v", 0), 14: ("v", 1)}


def shared_bank_order():
    order = [("q", 0, 0), ("k", 0, 0), ("q", 1, 0), ("k", 1, 0), ("v", 0, 0), ("v", 0, 1), ("max", 0, 0)]
    for n in range(BATCHES):
        i = n // 2
        for j in range(ITEMS):
            if j in POST and n >= 1:
                order.append((POST[j][0], n - 1, POST[j][1]))
            if n % 2 == 0 and j in EVEN:
                order.append((EVEN[j][0], i, EVEN[j][1]))
            if n % 2 == 1 and j in ODD:
                what, part = ODD[j]
                to = i + 2 if what in "qk" else i + 1
                if to < PAIRS:
                    order.append((what, to, part))
        if n + 1 < BATCHES:
            order.append(("max", n + 1, 0))
    for j in sorted(POST):
        order.append((POST[j][0], BATCHES - 1, POST[j][1]))
    return {use: at for at, use in enumerate(order)}


SHARED = shared_bank_order()
SHARED_PER_PAIR = 22


class Step:

    def __init__(self, ahead=None):
        self.ahead = ahead

    def value(self, at_ref, per_pair):
        return at_ref if self.ahead is None else at_ref + self.ahead * per_pair

    def wait(self, eng, sem, at_ref, per_pair):
        if self.ahead is not None or at_ref > 0:
            eng.wait_ge(sem, self.value(at_ref, per_pair))


class Count:

    def __init__(self, eng, sem):
        self.eng, self.sem, self.n, self.extra = eng, sem, 0, None

    def link(self, ins):
        ins.then_inc(self.sem, 1)
        self.n += 1
        self.eng.wait_ge(self.sem, self.n if self.extra is None else self.extra + self.n)

    def enter(self, turn, per_turn):
        self.extra, self.start, self.per_turn = turn * per_turn, self.n, per_turn

    def leave(self, turns):
        assert self.n - self.start == self.per_turn, (self.n - self.start, self.per_turn)
        self.n, self.extra = self.start + turns * self.per_turn, None


def build(nc, x, wq, bq, wk, bk, wv, bv, wo, bo, wr, wgu, wdn, wg, wu, wd, cst, mask_q, mask_k, tok, out):
    ctx = ExitStack()
    with ctx:
        def sb(name, shape, dt=F32):
            return ctx.enter_context(nc.sbuf_tensor(name, shape, dt))

        def sem(name):
            return ctx.enter_context(nc.semaphore(name))

        xnT_dram = nc.dram_tensor("xnT_keep", [PAIRS, P, PAIR], F32).ap()
        sorted_dram = nc.dram_tensor("sorted_keep", [SORTED * P, ROW], F32).ap()
        back_dram = nc.dram_tensor("back_keep", [TOKENS, D], F32).ap()

        x_res = sb("x_res", [P, TILES, D])
        stack_q = [sb(f"stack_q{b}", [P, HEADS, PAIR], BF16) for b in range(2)]
        stack_k = [sb(f"stack_k{b}", [P, HEADS, PAIR], BF16) for b in range(2)]
        gu_sb = sb("gu_sb", [P, EXPERTS * 2 * F])
        dn_sb = sb("dn_sb", [P, EXPERTS * 2 * D])
        v_sb = [sb(f"v_sb{b}", [P, PT, HEADS, DH + 1]) for b in range(2)]
        xnT = [sb(f"xnT{b}", [P, PAIR]) for b in range(2)]
        q32 = sb("q32", [P, PAIR])
        k32 = sb("k32", [P, PAIR])
        q_parts = sb("q_parts", [P, 3, PAIR], BF16)
        k_parts = sb("k_parts", [P, 3, PAIR], BF16)
        probs = sb("probs", [P, 4, 2, 160])
        att = sb("att", [P, 4, SEQ])
        att_n = sb("att_n", [P, 2, D])
        att_nT = sb("att_nT", [P, 2, P])
        recip = sb("recip", [P, 2, HEADS])
        neg_max = sb("neg_max", [P, 2, HEADS])
        max_parts = sb("max_parts", [P, 2, 3, HEADS], BF16)
        maxT = sb("maxT", [3 * HEADS, SEQ], BF16)
        th = sb("th", [P, PAIR])
        gated = sb("gated", [P, PAIR])
        hT = sb("hT", [P, 2, PAIR])
        wq_sb, wk_sb, wv_sb, wo_sb = (sb(n, [P, D]) for n in ("wq_sb", "wk_sb", "wv_sb", "wo_sb"))
        wr_sb = sb("wr_sb", [P, EXPERTS])
        wg_sb, wu_sb, wd_sb = (sb(n, [P, F]) for n in ("wg_sb", "wu_sb", "wd_sb"))
        bq_sb, bk_sb, bqs = (sb(n, [P, 1]) for n in ("bq_sb", "bk_sb", "bqs"))
        bv_sb, bo_sb = sb("bv_sb", [P, D]), sb("bo_sb", [P, D])
        cst_sb = sb("cst_sb", [P, cst.shape[1]])
        ident, before = cst_sb[:, 0:P], cst_sb[:, P:2 * P]
        rev = cst_sb[:, 2 * P:2 * P + EXPERTS]
        steps128 = cst_sb[:, 2 * P + EXPERTS:2 * P + EXPERTS + TILES]
        tile_no = cst_sb[:, 2 * P + EXPERTS + TILES:2 * P + EXPERTS + TILES + SORTED]
        ident_bf = sb("ident_bf", [P, P], BF16)
        mask_q_sb, mask_k_sb = sb("mask_q_sb", [P, SEQ], BF16), sb("mask_k_sb", [P, SEQ], BF16)
        tok_sb = sb("tok_sb", [P, TILES], I32)
        ones = sb("ones", [P, P])
        stats = sb("stats", [P, 2, PT, 6])
        moments = sb("moments", [P, 4, PT, 2])
        var_eps = sb("var_eps", [P, PT])
        neg_half = sb("neg_half", [P, PT])
        mean, rstd = sb("mean", [P, TILES]), sb("rstd", [P, TILES])
        slot = sb("slot", [P, TILES], I32)
        send_scale, send_shift = sb("send_scale", [P, TILES]), sb("send_shift", [P, TILES])
        send = sb("send", [P, 2, PT, ROW])
        expert_of = sb("expert_of", [P, SORTED + 4], I32)

        def scratch(at, *shape):
            n = int(np.prod(shape))
            ap = gu_sb[:, at:at + n]
            return ap if len(shape) == 1 else ap.rearrange("p (a b) -> p a b", b=shape[1])

        E, T = EXPERTS, TILES
        xn = [scratch(b * PAIR, PT, D) for b in range(2)]
        logits = scratch(1024, T, E)
        hot, tally_a, tally_b, work = (scratch(2048 + 1024 * k, T, E) for k in range(4))
        compare = scratch(6144, SORTED, E)
        small = [scratch(7424 + 80 * k, 80) for k in range(9)]
        top, first, score, row_count, n_tiles, ends_a, ends_b, base, slot_f = small
        late = stack_q[0][:, :, :].rearrange("p h n -> p (h n)").bitcast(F32)
        late2 = stack_k[0][:, :, :].rearrange("p h n -> p (h n)").bitcast(F32)
        ring = late[:, 0:8 * ROW].rearrange("p (r c) -> p r c", c=ROW)
        rowT = late[:, 1100:1100 + 2 * P].rearrange("p (r c) -> p r c", c=P)
        e_th = late[:, 1400:1400 + 2 * F].rearrange("p (r c) -> p r c", c=F)
        e_gated = late2[:, 2100:2100 + 2 * F].rearrange("p (r c) -> p r c", c=F)
        e_h = late[:, 2300:2300 + 2 * F].rearrange("p (r c) -> p r c", c=F)
        e_hT = late[:, 2900:2900 + 2 * F].rearrange("p (r c) -> p r c", c=F)
        e_y = late[:, 3500:3500 + 4 * D].rearrange("p (r c) -> p r c", c=D)
        fetched = late2[:, 0:4 * PT * D].rearrange("p (r t d) -> p r t d", r=4, d=D)

        bank = [ctx.enter_context(nc.psum_tensor(f"bank{b}", [P, 512], F32)) for b in range(8)]
        first_bank, second_bank, att_bank, shared_bank = bank[0:2], bank[2:4], bank[4:6], bank[6:8]

        x_loaded = [sem(f"x_loaded{b}") for b in range(2)]
        const_loaded, weights_loaded = sem("const_loaded"), sem("weights_loaded")
        masks_loaded, stacks_masked = sem("masks_loaded"), sem("stacks_masked")
        blank_made, blanks_stored = sem("blank_made"), sem("blanks_stored")
        prepared, waits_passed = sem("prepared"), sem("waits_passed")
        stats_done, moments_done, rstd_done = sem("stats_done"), sem("moments_done"), sem("rstd_done")
        xn_done, xn_turned, xnT_done = sem("xn_done"), sem("xn_turned"), sem("xnT_done")
        xnT_stored = [sem(f"xnT_stored{b}") for b in range(2)]
        logits_out, logits_done = sem("logits_out"), sem("logits_done")
        top_done, exp_top_done, counted, ranked, routed = (
            sem(n) for n in ("top_done", "exp_top_done", "counted", "ranked", "routed"))
        dve_own, pool_own = sem("dve_own"), sem("pool_own")
        send_made = sem("send_made")
        sent = [sem(f"sent{b}") for b in range(2)]
        experts_loaded = sem("experts_loaded")
        xnT_loaded = [sem(f"xnT_loaded{b}") for b in range(2)]
        parts_made = sem("parts_made")
        stack_loaded = [sem(f"stack_loaded{b}") for b in range(2)]
        first_out, max_taken = sem("first_out"), sem("max_taken")
        second_out, exp_done, att_added, att_taken = (
            sem(n) for n in ("second_out", "exp_done", "att_added", "att_taken"))
        shared_out = [sem(f"shared_out{b}") for b in range(2)]
        shared_used = [sem(f"shared_used{b}") for b in range(2)]
        max_split, max_loaded = sem("max_split"), sem("max_loaded")
        recip_done, tanh_done, bo_added = sem("recip_done"), sem("tanh_done"), sem("bo_added")
        row_loaded = [sem(f"row_loaded{r}") for r in range(8)]
        row_turned, rowT_done, gu_out, e_tanh_done, e_gated_done, h_done = (
            sem(n) for n in ("row_turned", "rowT_done", "gu_out", "e_tanh_done", "e_gated_done", "h_done"))
        h_turned, e_hT_done, y_out, y_done = (sem(n) for n in ("h_turned", "e_hT_done", "y_out", "y_done"))
        y_sent = [sem(f"y_sent{r}") for r in range(4)]
        back_loaded = [sem(f"back_loaded{r}") for r in range(4)]
        all_added, out_stored = sem("all_added"), sem("out_stored")

        block = ctx.enter_context(nc.Block())

        x_by_chunk = x.rearrange("(c k p) d -> c p k d", p=P, k=PT)
        out_by_chunk = out.rearrange("(c k p) d -> c p k d", p=P, k=PT)
        back_by_chunk = back_dram.rearrange("(c k p) d -> c p k d", p=P, k=PT)

        def shared(what, of, part, step):
            at = SHARED[(what, of, part)]
            return at % 2, step.value(at // 2, SHARED_PER_PAIR // 2)

        def shared_wait_free(eng, what, of, part, step):
            b, _ = shared(what, of, part, step)
            step.wait(eng, shared_used[b], SHARED[(what, of, part)] // 2, SHARED_PER_PAIR // 2)
            return b

        def shared_wait_out(eng, what, of, part, step):
            b, _ = shared(what, of, part, step)
            step.wait(eng, shared_out[b], SHARED[(what, of, part)] // 2 + 1, SHARED_PER_PAIR // 2)
            return b

        def shared_wait_used(eng, what, of, part, step):
            b, _ = shared(what, of, part, step)
            step.wait(eng, shared_used[b], SHARED[(what, of, part)] // 2 + 1, SHARED_PER_PAIR // 2)

        def over_pairs(eng, emit, count=None, per_turn=0):
            for i in (0, 1):
                emit(i, Step())
            with eng.Fori(0, 6) as turn:
                if count:
                    count.enter(turn, per_turn)
                for i in (2, 3):
                    emit(i, Step(turn * 2))
            if count:
                count.leave(6)
            for i in (14, 15):
                emit(i, Step())

        def over_sorted(eng, emit):
            for s in range(8):
                emit(s, None)
            with eng.Fori(0, SORTED // 8 - 2) as turn:
                for s in range(8, 16):
                    emit(s, turn * 8)
            for s in range(SORTED - 8, SORTED):
                emit(s, None)

        def pass_wait(eng):
            eng.sem_inc(waits_passed, 1)

        def plus(value, ahead, factor=1):
            return value if ahead is None else value + (ahead if factor == 1 else ahead * factor)

        def wait_count(eng, s, value, ahead):
            if ahead is not None or value > 0:
                eng.wait_ge(s, plus(value, ahead))

        @block.sync
        def _(sp):
            def load_x(c, half, b, to):
                if to is None or to > 0:
                    sp.wait_ge(x_loaded[b], half)
                    pass_wait(sp)
                sp.dma_start(x_res[:, bass.ds(c * PT, PT), :] if to is None else x_res[:, c * PT:c * PT + PT, :],
                             x_by_chunk[bass.ds(c, 1), :, :, :].rearrange("a p k d -> (a p) k d") if to is None else x_by_chunk[c]).then_inc(x_loaded[b], 16)

            for c in (0, 1):
                load_x(c, 0, c, 0)
            with sp.Fori(1, PAIRS // 2) as k:
                for b in range(2):
                    load_x(k * 2 + b, k * 16, b, None)
            sp.wait_ge(masks_loaded, 32)
            for b in range(2):
                for stack, mask in ((stack_q, mask_q_sb), (stack_k, mask_k_sb)):
                    sp.dma_start(stack[b][:, :, :].rearrange("p h (u n) -> p (h u) n", u=2),
                                 mask[:, :].unsqueeze(1).to_broadcast([P, 2 * HEADS, SEQ])).then_inc(stacks_masked, 16)

            def load_xnT(i, step):
                if i >= 2:
                    shared_wait_out(sp, "up", i - 2, 1, step)
                    pass_wait(sp)
                src = xnT_dram[i] if step.ahead is None else xnT_dram[bass.ds(step.ahead + i, 1), :, :].rearrange("a p n -> (a p) n")
                sp.dma_start(xnT[i % 2][:, :], src).then_inc(xnT_loaded[i % 2], 16)

            def stack_parts(i, step):
                step.wait(sp, parts_made, 2 * i + 2, 2)
                pass_wait(sp)
                step.wait(sp, second_out, 2 * ITEMS * (i - 1), 2 * ITEMS)
                pass_wait(sp)
                for stack, parts, which in ((stack_q, q_parts, Q_PARTS), (stack_k, k_parts, K_PARTS)):
                    for row, part in zip(PART_ROWS, which):
                        sp.dma_start(stack[i % 2][row:row + DH, :, :], parts[:, part, :]).then_inc(stack_loaded[i % 2], 16)

            def stack_max(n, step):
                shared_wait_used(sp, "max", n, 0, step)
                half = (n % 2) * SEQ
                for part in range(3):
                    sp.dma_start(stack_q[(n // 2) % 2][MAX_ROW + part:MAX_ROW + part + 1, :, half:half + SEQ],
                                 maxT[HEADS * part:HEADS * part + HEADS, :]).then_inc(max_loaded, 16)

            for b in range(2):
                sp.wait_ge(xnT_stored[b], 16 * (PAIRS // 2))
            sp.wait_ge(stacks_masked, 64)
            sp.wait_ge(logits_out, PAIRS)
            plain = Step()
            load_xnT(0, plain)
            load_xnT(1, plain)
            stack_parts(0, plain)
            stack_parts(1, plain)
            sp.wait_ge(routed, 1)
            sp.dma_start(gu_sb[:, :].rearrange("p (e f) -> p e f", e=EXPERTS), wgu.rearrange("e p f -> p e f")).then_inc(experts_loaded, 16)
            sp.dma_start(dn_sb[:, :].rearrange("p (e u d) -> p e u d", e=EXPERTS, u=2), wdn.rearrange("e (u p) d -> p e u d", p=P)).then_inc(experts_loaded, 16)
            stack_max(0, plain)

            def pair(i, step):
                if 1 <= i < PAIRS - 1:
                    stack_parts(i + 1, step)
                if i + 2 < PAIRS:
                    load_xnT(i + 2, step)
                stack_max(2 * i + 1, step)
                if i + 1 < PAIRS:
                    stack_max(2 * i + 2, step)

            over_pairs(sp, pair)

            sp.wait_ge(att_added, ITEMS * BATCHES)
            for b in range(2):
                sp.wait_ge(sent[b], 16 * TILES // 2)
            by_tile = sorted_dram.rearrange("(s p) c -> s p c", p=P)

            def load_row(s, ahead):
                if ahead is not None or s >= 8:
                    sp.wait_ge(y_sent[s % 4], plus((s - 8) // 4 * 16 + 16, ahead, 4))
                    pass_wait(sp)
                src = by_tile[s] if ahead is None else by_tile[bass.ds(ahead + s, 1), :, :].rearrange("a p c -> (a p) c")
                sp.dma_start(ring[:, s % 8, :], src).then_inc(row_loaded[s % 8], 16)

            over_sorted(sp, load_row)

            for r in range(4):
                sp.wait_ge(y_sent[r], 16 * SORTED // 4)

            def load_back(c, ahead):
                if ahead is not None:
                    sp.wait_ge(all_added, plus(c - 3, ahead))
                    pass_wait(sp)
                src = back_by_chunk[c] if ahead is None else back_by_chunk[bass.ds(ahead + c, 1), :, :, :].rearrange("a p k d -> (a p) k d")
                sp.dma_start(fetched[:, c % 4, :, :], src).then_inc(back_loaded[c % 4], 16)

            for c in range(4):
                load_back(c, None)
            with sp.Fori(0, PAIRS // 4 - 1) as turn:
                for c in range(4, 8):
                    load_back(c, turn * 4)
            sp.wait_ge(out_stored, 16 * PAIRS)

        @block.gpsimd
        def _(pool):
            own = Count(pool, pool_own)
            blank = send[:, 0:2, :, :].rearrange("p a b c -> p (a b) c")
            nc.gpsimd.memset(blank[:, :, 0:D], 0.0)
            nc.gpsimd.memset(blank[:, :, D:ROW].bitcast(I32), TOKENS).then_inc(blank_made, 1)
            own.link(nc.gpsimd.memset(neg_half[:, :], -0.5))
            for c in range(PAIRS):
                t = slice(c * PT, c * PT + PT)
                pool.wait_ge(moments_done, c + 1)
                if c >= 1:
                    pool.wait_ge(rstd_done, c)
                own.link(nc.gpsimd.tensor_scalar(var_eps[:, :], moments[:, c % 4, :, 1], 1.0, EPS, ALU.mult, ALU.add))
                nc.gpsimd.tensor_copy(mean[:, t], moments[:, c % 4, :, 0])
                nc.gpsimd.tensor_tensor(rstd[:, t], var_eps[:, :], neg_half[:, :], ALU.pow).then_inc(rstd_done, 1)

            plain = Step()

            def split(i):
                for k, (full, parts) in enumerate(((q32, q_parts), (k32, k_parts))):
                    shared_wait_used(pool, "qk"[k], i, 0, plain)
                    own.link(nc.gpsimd.tensor_tensor(full[:, :], full[:, :], parts[:, 0, :], ALU.subtract))
                    own.link(nc.gpsimd.tensor_scalar(parts[:, 1, :], full[:, :], 1.0, 0.0, ALU.mult, ALU.add))
                    nc.gpsimd.tensor_tensor(parts[:, 2, :], full[:, :], parts[:, 1, :], ALU.subtract).then_inc(parts_made, 1)

            def scatter(g):
                b = g % 2
                if g == 0:
                    pool.wait_ge(blanks_stored, 16 * (SORTED // 8))
                    pool.wait_ge(routed, 1)
                    for k in range(2):
                        pool.wait_ge(x_loaded[k], 16 * (PAIRS // 2))
                if g >= 2:
                    pool.wait_ge(sent[b], 16 * PT * (g // 2))
                for k in range(PT):
                    t = g * PT + k
                    nc.gpsimd.tensor_scalar(send[:, b, k, 0:D], x_res[:, t, :], send_scale[:, t:t + 1],
                                            send_shift[:, t:t + 1], ALU.mult, ALU.add)
                nc.gpsimd.tensor_copy(send[:, b, :, D:D + 1].bitcast(I32),
                                      tok_sb[:, g * PT:g * PT + PT].unsqueeze(2)).then_inc(send_made, 1)
                pool.wait_ge(send_made, g + 1)
                for k in range(PT):
                    t = g * PT + k
                    nc.gpsimd.indirect_dma_start(
                        sorted_dram, bass.IndirectOffsetOnAxis(slot[:, t:t + 1].bitcast(U32), 0),
                        send[:, b, k, :], None, bounds_check=SORTED * P - 1, oob_is_err=False).then_inc(sent[b], 16)

            def add_bo(i):
                for n in (2 * i, 2 * i + 1):
                    for qt in range(2):
                        shared_wait_used(pool, "sum", n, qt, plain)
                t = slice(i * PT, i * PT + PT)
                nc.gpsimd.tensor_tensor(x_res[:, t, :], x_res[:, t, :], bo_sb[:, :].unsqueeze(1).to_broadcast([P, PT, D]),
                                        ALU.add).then_inc(bo_added, 1)

            split(0)
            split(1)
            for i in range(PAIRS):
                scatter(i)
                if i + 2 < PAIRS:
                    split(i + 2)
                if i >= 1:
                    add_bo(i - 1)
            add_bo(PAIRS - 1)

            def send_back(s, ahead):
                pool.wait_ge(y_done, plus(s + 1, ahead))
                pass_wait(pool)
                nc.gpsimd.indirect_dma_start(
                    back_dram, bass.IndirectOffsetOnAxis(ring[:, s % 8, D:D + 1].bitcast(U32), 0),
                    e_y[:, s % 4, :], None, bounds_check=TOKENS - 1, oob_is_err=False).then_inc(y_sent[s % 4], 16)

            over_sorted(pool, send_back)

        @block.scalar
        def _(act):
            act.dma_start(cst_sb[:, :], cst).then_inc(const_loaded, 16)
            act.dma_start(wr_sb[:, :], wr).then_inc(const_loaded, 16)
            act.dma_start(mask_q_sb[:, :].bitcast(U16), mask_q).then_inc(masks_loaded, 16)
            act.dma_start(mask_k_sb[:, :].bitcast(U16), mask_k).then_inc(masks_loaded, 16)
            loads = [(wq_sb[:, :], wq), (wk_sb[:, :], wk), (wv_sb[:, :], wv), (wo_sb[:, :], wo), (wg_sb[:, :], wg),
                     (wu_sb[:, :], wu), (wd_sb[:, :].rearrange("p (u d) -> p u d", u=2), wd.rearrange("(u p) d -> p u d", p=P)),
                     (bq_sb[:, :], bq), (bk_sb[:, :], bk), (bv_sb[:, :], bv.to_broadcast([P, D])),
                     (bo_sb[:, :], bo.to_broadcast([P, D])), (tok_sb[:, :], tok)]
            for dst, src in loads:
                act.dma_start(dst, src).then_inc(weights_loaded, 16)

            def take_xnT(c, b, half, runtime):
                act.wait_ge(xn_turned, c + 1)
                if runtime:
                    act.wait_ge(logits_out, c - 1)
                    act.wait_ge(xnT_stored[b], half * 16)
                act.activation(xnT[b][:, :], first_bank[b][:, :], ACT.Copy).then_inc(xnT_done, 1)
                act.wait_ge(xnT_done, c + 1)
                dst = xnT_dram[bass.ds(c, 1), :, :].rearrange("a p n -> (a p) n") if runtime else xnT_dram[c]
                act.dma_start(dst, xnT[b][:, :]).then_inc(xnT_stored[b], 16)

            def take_logits(c, b, runtime):
                act.wait_ge(logits_out, c + 1)
                dst = logits[:, bass.ds(c * PT, PT), :] if runtime else logits[:, c * PT:c * PT + PT, :]
                act.activation(dst, second_bank[b][:, 0:PT * E].rearrange("p (t e) -> p t e", e=E), ACT.Copy).then_inc(logits_done, 1)

            take_xnT(0, 0, 0, False)
            take_xnT(1, 1, 0, False)
            take_logits(0, 0, False)
            blank = send[:, 0:2, :, :].rearrange("p a b c -> p (a b) c")
            act.wait_ge(blank_made, 1)
            for k in range(SORTED // 8):
                act.dma_start(sorted_dram[k * 8 * P:(k + 1) * 8 * P, :].rearrange("(p r) c -> p r c", p=P), blank).then_inc(blanks_stored, 16)
            with act.Fori(1, PAIRS // 2) as k:
                take_xnT(k * 2, 0, k, True)
                take_logits(k * 2 - 1, 1, True)
                take_xnT(k * 2 + 1, 1, k, True)
                take_logits(k * 2, 0, True)
            take_logits(PAIRS - 1, 1, False)

            act.wait_ge(top_done, 1)
            act.activation(score[:, 0:T], top[:, 0:T], ACT.Exp, scale=-1.0).then_inc(exp_top_done, 1)

            def take_qk(what, i, step):
                b = shared_wait_out(act, what, i, 0, step)
                if what == "q":
                    step.wait(act, parts_made, 2 * i, 2)
                    if i >= 1:
                        step.wait(act, stack_loaded[(i - 1) % 2], 192 * ((i - 1) // 2 + 1), 96)
                full, parts, scale, bias = ((q32, q_parts, DH**-0.5, bqs) if what == "q" else (k32, k_parts, 1.0, bk_sb))
                act.activation(parts[:, 0, :], shared_bank[b][:, :], ACT.Identity, bias=bias[:, :], scale=scale)
                act.activation(full[:, :], shared_bank[b][:, :], ACT.Identity, bias=bias[:, :], scale=scale).then_inc(shared_used[b], 1)

            def take_max(n, step):
                b = shared_wait_out(act, "max", n, 0, step)
                step.wait(act, max_loaded, 48 * n, 96)
                act.activation(maxT[:, :], shared_bank[b][0:3 * HEADS, 0:SEQ // 2].bitcast(BF16), ACT.Copy).then_inc(shared_used[b], 1)

            def take_att(n, half, step):
                step.wait(act, att_added, ITEMS * n + 8 * (half + 1), 2 * ITEMS)
                for qt in range(2 if n >= 1 else 0):
                    shared_wait_out(act, "turn", n - 1, qt, step)
                act.activation(att[:, 2 * half:2 * half + 2, :].rearrange("p s n -> p (s n)"), att_bank[half][:, :],
                               ACT.Copy).then_inc(att_taken, 1)

            def batch(n, i, step, items=True):
                for j in range(ITEMS + 2):
                    if items and j < ITEMS:
                        width = K_ITEM[j % 2][2]
                        step.wait(act, second_out, ITEMS * n + j + 1, 2 * ITEMS)
                        step.wait(act, att_added, ITEMS * n + j - 3, 2 * ITEMS)
                        act.activation(probs[:, j % 4, :, 0:width],
                                       second_bank[j % 2][:, :].rearrange("p (u w) -> p u w", u=2)[:, :, 0:width],
                                       ACT.Exp).then_inc(exp_done, 1)
                    if j == 0 and n >= 1:
                        take_att(n - 1, 1, step)
                    if j == 11 and items:
                        take_att(n, 0, step)
                    if n >= 1 and j in (7, 8):
                        qt = j - 7
                        b = shared_wait_out(act, "back", n - 1, qt, step)
                        if n >= 2:
                            shared_wait_used(act, "sum", n - 2, qt, step)
                        act.activation(att_nT[:, qt, :], shared_bank[b][:, 0:P], ACT.Copy).then_inc(shared_used[b], 1)
                    if items and n % 2 == 0 and j in (12, 14):
                        f = (j - 12) // 2
                        b = shared_wait_out(act, "gate", i, f, step)
                        if i + f >= 1:
                            shared_wait_used(act, "gate", i + f - 1, 1 - f, step)
                        act.activation(th[:, :], shared_bank[b][:, :], ACT.Tanh, scale=0.5).then_inc(tanh_done, 1)
                    if items and n % 2 == 1 and i + 2 < PAIRS and j in (12, 13):
                        take_qk("q" if j == 12 else "k", i + 2, step)
                if items and n + 1 < BATCHES:
                    take_max(n + 1, step)

            plain = Step()
            for i in (0, 1):
                take_qk("q", i, plain)
                take_qk("k", i, plain)
            take_max(0, plain)

            def pair(i, step):
                batch(2 * i, i, step)
                batch(2 * i + 1, i, step)

            over_pairs(act, pair)
            batch(BATCHES, PAIRS, plain, items=False)

            def expert_tile(s, ahead):
                def take_row(s):
                    wait_count(act, row_turned, s + 1, ahead)
                    wait_count(act, gu_out, s - 1, ahead)
                    act.activation(rowT[:, s % 2, :], second_bank[s % 2][:, 0:P], ACT.Copy).then_inc(rowT_done, 1)

                if s == 0 and ahead is None:
                    take_row(0)
                if s + 1 < SORTED or ahead is not None:
                    take_row(s + 1)
                wait_count(act, gu_out, s + 1, ahead)
                wait_count(act, e_gated_done, s - 1, ahead)
                act.activation(e_th[:, s % 2, :], first_bank[s % 2][:, 0:F], ACT.Tanh, scale=0.5).then_inc(e_tanh_done, 1)

                def take_h(s):
                    wait_count(act, h_turned, s + 1, ahead)
                    wait_count(act, y_out, s - 1, ahead)
                    act.activation(e_hT[:, s % 2, :], att_bank[s % 2][:, 0:F], ACT.Copy, scale=0.5).then_inc(e_hT_done, 1)

                if s >= 1:
                    take_h(s - 1)
                if s == SORTED - 1:
                    take_h(s)

            over_sorted(act, expert_tile)

            for c in range(PAIRS):
                act.wait_ge(all_added, c + 1)
                act.dma_start(out_by_chunk[c], x_res[:, c * PT:c * PT + PT, :]).then_inc(out_stored, 16)

        @block.tensor
        def _(pe):
            pe.wait_ge(const_loaded, 32)

            def norm_chunk(c, b, runtime):
                pe.wait_ge(xn_done, c + 1)
                if runtime:
                    pe.wait_ge(xnT_done, c - 1)
                for k in range(PT):
                    last = nc.tensor.transpose(first_bank[b][:, k * P:(k + 1) * P], xn[b][:, k, :], ident)
                last.then_inc(xn_turned, 1)
                pe.wait_ge(xnT_done, c + 1)
                if runtime:
                    pe.wait_ge(logits_done, c - 1)
                for k in range(PT):
                    last = nc.tensor.matmul(second_bank[b][:, k * E:(k + 1) * E], xnT[b][:, k * P:(k + 1) * P],
                                            wr_sb[:, :], start=True, stop=True)
                last.then_inc(logits_out, 1)

            norm_chunk(0, 0, False)
            norm_chunk(1, 1, False)
            with pe.Fori(1, PAIRS // 2) as k:
                norm_chunk(k * 2, 0, True)
                norm_chunk(k * 2 + 1, 1, True)

            pe.wait_ge(weights_loaded, 16 * 12)
            pe.wait_ge(prepared, 1)

            def project(what, i, step):
                b = shared_wait_free(pe, what, i, 0, step)
                step.wait(pe, xnT_loaded[i % 2], 16 * (i // 2 + 1), 8)
                nc.tensor.matmul(shared_bank[b][:, :], (wq_sb if what == "q" else wk_sb)[:, :], xnT[i % 2][:, :],
                                 start=True, stop=True).then_inc(shared_out[b], 1)

            def project_v(i, half, step):
                b = shared_wait_free(pe, "v", i, half, step)
                for k in (2 * half, 2 * half + 1):
                    last = nc.tensor.matmul(shared_bank[b][:, (k % 2) * D:(k % 2 + 1) * D], xnT[i % 2][:, k * P:(k + 1) * P],
                                            wv_sb[:, :], start=True, stop=True)
                last.then_inc(shared_out[b], 1)

            def gate_up(what, i, f, step):
                b = shared_wait_free(pe, what, i, f, step)
                w = wg_sb if what == "gate" else wu_sb
                last = nc.tensor.matmul(shared_bank[b][:, :], w[:, f * P:(f + 1) * P], xnT[i % 2][:, :], start=True, stop=True)
                last.then_inc(shared_out[b], 1)

            def first_scores(n, j, step):
                (q0, k0, width), i = Q_ITEM[j % 2], n // 2
                if j == 0 and n % 2 == 0:
                    step.wait(pe, stack_loaded[i % 2], 192 * (i // 2 + 1), 96)
                step.wait(pe, max_taken, ITEMS * n + j - 1, 2 * ITEMS)
                at = (n % 2) * SEQ
                for u in range(2):
                    h = 2 * (j // 2) + u
                    last = nc.tensor.matmul(first_bank[j % 2][:, u * 256:u * 256 + width],
                                            stack_q[i % 2][0:ROWS_Q, h, at + q0:at + q0 + P],
                                            stack_k[i % 2][0:ROWS_Q, h, at + k0:at + k0 + width], start=True, stop=True)
                last.then_inc(first_out, 1)

            def second_scores(n, j, step):
                (k0, q0, width), i = K_ITEM[j % 2], n // 2
                if j == 0:
                    step.wait(pe, max_loaded, 48 * (n + 1), 96)
                step.wait(pe, exp_done, ITEMS * n + j - 1, 2 * ITEMS)
                at = (n % 2) * SEQ
                for u in range(2):
                    h = 2 * (j // 2) + u
                    last = nc.tensor.matmul(second_bank[j % 2][:, u * 256:u * 256 + width],
                                            stack_k[i % 2][0:ROWS_K, h, at + k0:at + k0 + P],
                                            stack_q[i % 2][0:ROWS_K, h, at + q0:at + q0 + width], start=True, stop=True)
                last.then_inc(second_out, 1)

            def add_values(n, j, step):
                (_, q0, width), i = K_ITEM[j % 2], n // 2
                step.wait(pe, exp_done, ITEMS * n + j + 1, 2 * ITEMS)
                if j == 0:
                    if n % 2 == 0:
                        for half in range(2):
                            shared_wait_used(pe, "v", i, half, step)
                    step.wait(pe, att_taken, 2 * n - 1, 4)
                if j == 8:
                    step.wait(pe, att_taken, 2 * n, 4)
                for u in range(2):
                    h = 2 * (j // 2) + u
                    row, col = 32 * (h % 4), SEQ * (h // 4 % 2) + q0
                    last = nc.tensor.matmul(att_bank[h // 8][row:row + DH + 1, col:col + width],
                                            v_sb[i % 2][:, 2 * (n % 2) + j % 2, h, :], probs[:, j % 4, u, 0:width],
                                            start=(j % 2 == 0), stop=(j % 2 == 1), skip_group_check=True)
                last.then_inc(att_added, 1)

            def turn(n, qt, step):
                b = shared_wait_free(pe, "turn", n, qt, step)
                step.wait(pe, att_taken, 2 * n + 2, 4)
                for s in range(4):
                    last = nc.tensor.transpose(shared_bank[b][:, s * P:(s + 1) * P], att[:, s, qt * P:(qt + 1) * P], ident)
                last.then_inc(shared_out[b], 1)

            def back(n, qt, step):
                b = shared_wait_free(pe, "back", n, qt, step)
                assert SHARED[("back", n, qt)] == SHARED[("turn", n, qt)] + 2
                nc.tensor.transpose(shared_bank[b][:, 0:P], att_n[:, qt, :], ident).then_inc(shared_out[b], 1)

            def sum_rest(n, qt, step):
                b = shared_wait_free(pe, "sum", n, qt, step)
                assert SHARED[("sum", n, qt)] == SHARED[("back", n, qt)] + 2
                for f in range(2):
                    assert (SHARED[("sum", n // 2 * 2, 0)] - SHARED[("up", n // 2, f)]) % 2 == 0
                nc.tensor.matmul(shared_bank[b][:, 0:D], att_nT[:, qt, :], wo_sb[:, :], start=True, stop=False)
                at = (n % 2) * SEQ + qt * P
                for f in range(2):
                    last = nc.tensor.matmul(shared_bank[b][:, 0:D], hT[:, f, at:at + P], wd_sb[:, f * D:(f + 1) * D],
                                            start=False, stop=(f == 1))
                last.then_inc(shared_out[b], 1)

            def turn_max(n, step):
                step.wait(pe, max_split, n + 1, 2)
                b = shared_wait_free(pe, "max", n, 0, step)
                pass_wait(pe)
                view = shared_bank[b][:, :].bitcast(BF16)
                for qt in range(2):
                    last = nc.tensor.transpose(view[0:3 * HEADS, qt * P:(qt + 1) * P],
                                               max_parts[:, qt, :, :].rearrange("p a h -> p (a h)"), ident_bf[:, :])
                last.then_inc(shared_out[b], 1)

            post = {"turn": turn, "back": back, "sum": sum_rest}
            plain = Step()
            for i in (0, 1):
                project("q", i, plain)
                project("k", i, plain)
            project_v(0, 0, plain)
            project_v(0, 1, plain)
            pe.wait_ge(counted, 1)
            nc.tensor.matmul(second_bank[0][:, 0:E], before, row_count[:, 0:E], start=True, stop=True)
            nc.tensor.matmul(second_bank[0][:, E:2 * E], ones[:, :], row_count[:, 0:E], start=True, stop=True).then_inc(ranked, 1)
            pe.wait_ge(routed, 1)
            for j in range(ITEMS):
                first_scores(0, j, plain)
            turn_max(0, plain)

            def batch(n, i, step):
                for j in range(ITEMS + 2):
                    if j < ITEMS:
                        if n + 1 < BATCHES:
                            first_scores(n + 1, j, step)
                        second_scores(n, j, step)
                    if j >= 2:
                        add_values(n, j - 2, step)
                    if j < ITEMS:
                        if j in POST and n >= 1:
                            post[POST[j][0]](n - 1, POST[j][1], step)
                        if n % 2 == 0 and j in EVEN:
                            gate_up(EVEN[j][0], i, EVEN[j][1], step)
                        if n % 2 == 1 and j in ODD:
                            what, part = ODD[j]
                            if what == "v" and i + 1 < PAIRS:
                                project_v(i + 1, part, step)
                            elif what in "qk" and i + 2 < PAIRS:
                                project(what, i + 2, step)
                if n + 1 < BATCHES:
                    turn_max(n + 1, step)

            def pair(i, step):
                batch(2 * i, i, step)
                batch(2 * i + 1, i, step)

            over_pairs(pe, pair)
            for j in sorted(POST):
                post[POST[j][0]](BATCHES - 1, POST[j][1], plain)

            pe.wait_ge(experts_loaded, 32)

            experts = {}

            def expert_tile(s, ahead):
                if s % 8 == 0:
                    at = expert_of[0:1, s:s + 10] if ahead is None else expert_of[0:1, bass.ds(ahead + s, 10)]
                    _, got = nc.values_load_multi_w_load_instructions(at, engines=[pe.engine], min_val=0, max_val=EXPERTS - 1)
                    experts.update({s - 2 + k: e for k, e in enumerate(got)})

                def turn_row(s):
                    if ahead is None:
                        pe.wait_ge(row_loaded[s % 8], 16 * (s // 8 + 1))
                    else:
                        pe.wait_ge(row_loaded[s % 8], ahead * 2 + 16 * (s // 8 + 1))
                    wait_count(pe, rowT_done, s - 1, ahead)
                    nc.tensor.transpose(second_bank[s % 2][:, 0:P], ring[:, s % 8, 0:D], ident).then_inc(row_turned, 1)

                def turn_h(s):
                    wait_count(pe, h_done, s + 1, ahead)
                    wait_count(pe, e_hT_done, s - 1, ahead)
                    for f in range(2):
                        last = nc.tensor.transpose(att_bank[s % 2][:, f * P:(f + 1) * P], e_h[:, s % 2, f * P:(f + 1) * P], ident)
                    last.then_inc(h_turned, 1)

                def down(s):
                    wait_count(pe, e_hT_done, s + 1, ahead)
                    wait_count(pe, y_done, s - 1, ahead)
                    for f in range(2):
                        last = nc.tensor.matmul(shared_bank[s % 2][:, 0:D], e_hT[:, s % 2, f * P:(f + 1) * P],
                                                dn_sb[:, bass.ds(experts[s] * (2 * D) + f * D, D)], start=(f == 0), stop=(f == 1))
                    last.then_inc(y_out, 1)

                if s == 0 and ahead is None:
                    turn_row(0)
                if s + 1 < SORTED:
                    turn_row(s + 1)
                wait_count(pe, rowT_done, s + 1, ahead)
                wait_count(pe, h_done, s - 1, ahead)
                nc.tensor.matmul(first_bank[s % 2][:, :], rowT[:, s % 2, :], gu_sb[:, bass.ds(experts[s] * (2 * F), 2 * F)],
                                 start=True, stop=True).then_inc(gu_out, 1)
                if s >= 1:
                    turn_h(s - 1)
                if s >= 2:
                    down(s - 2)
                if s == SORTED - 1:
                    turn_h(s)
                    down(s - 1)
                    down(s)

            over_sorted(pe, expert_tile)

        @block.vector
        def _(dve):
            own = Count(dve, dve_own)
            nc.vector.memset(ones[:, :], 1.0)
            for b in range(2):
                nc.vector.memset(att_bank[b][:, :], 0.0)
                nc.vector.memset(v_sb[b][:, :, :, :], 1.0)
            nc.vector.memset(expert_of[:, :], 0)

            def take_stats(c, half, b, ring4, runtime):
                dve.wait_ge(x_loaded[b], half)
                for k in range(PT):
                    src = x_res[:, bass.ds(c * PT + k, 1), :] if runtime else x_res[:, c * PT + k:c * PT + k + 1, :]
                    last = nc.vector.bn_stats(stats[:, b, k, :], src.rearrange("p a d -> p (a d)"))
                last.then_inc(stats_done, 1)
                dve.wait_ge(stats_done, c + 1)
                pass_wait(dve)
                for k in range(PT):
                    last = nc.vector.bn_aggr(moments[:, ring4, k, :], stats[:, b, k, :])
                last.then_inc(moments_done, 1)

            def norm(c, b, ring4, runtime):
                dve.wait_ge(rstd_done, c + 1)
                if runtime or c >= 2:
                    dve.wait_ge(xn_turned, c - 1)
                for k in range(PT):
                    t = c * PT + k
                    src = x_res[:, bass.ds(t, 1), :].rearrange("p a d -> p (a d)") if runtime else x_res[:, t, :]
                    r = rstd[:, bass.ds(t, 1)] if runtime else rstd[:, t:t + 1]
                    last = nc.vector.tensor_scalar(xn[b][:, k, :], src, moments[:, ring4, k, 0:1], r, ALU.subtract, ALU.mult)
                last.then_inc(xn_done, 1)

            for c in range(4):
                take_stats(c, 16 * (c // 2 + 1), c % 2, c % 4, False)
                if c >= 1:
                    norm(c - 1, (c - 1) % 2, (c - 1) % 4, False)
            with dve.Fori(0, PAIRS // 4 - 1) as turn:
                for c in range(4, 8):
                    take_stats(turn * 4 + c, turn * 32 + 16 * (c // 2 + 1), c % 2, c % 4, True)
                    norm(turn * 4 + (c - 1), (c - 1) % 2, (c - 1) % 4, True)
            norm(PAIRS - 1, 1, 3, False)

            dve.wait_ge(weights_loaded, 16 * 12)
            nc.vector.tensor_scalar(bqs[:, :], bq_sb[:, :], DH**-0.5, None, ALU.mult)
            nc.vector.tensor_copy(ident_bf[:, :], ident).then_inc(prepared, 1)

            def take_v(i, half, step):
                b = shared_wait_out(dve, "v", i, half, step)
                dst = v_sb[i % 2][:, 2 * half:2 * half + 2, :, 0:DH]
                for k in range(2):
                    last = nc.vector.tensor_tensor(v_sb[i % 2][:, 2 * half + k, :, 0:DH],
                                                   shared_bank[b][:, k * D:(k + 1) * D].rearrange("p (h d) -> p h d", d=DH),
                                                   bv_sb[:, :].rearrange("p (h d) -> p h d", d=DH), ALU.add)
                last.then_inc(shared_used[b], 1)

            def over_experts(ap):
                return ap.unsqueeze(2).to_broadcast([P, T, E])

            def over_tiles(ap):
                return ap.unsqueeze(1).to_broadcast([P, T, E])

            plain = Step()
            dve.wait_ge(logits_done, PAIRS)
            top_ins = nc.vector.tensor_reduce(top[:, 0:T], logits, AX.X, ALU.max)
            top_ins.then_inc(top_done, 1)
            dve.wait_ge(top_done, 1)
            own.link(nc.vector.tensor_tensor(work, logits, over_experts(top[:, 0:T]), ALU.is_equal))
            own.link(nc.vector.tensor_tensor(work, work, over_tiles(rev), ALU.mult))
            own.link(nc.vector.tensor_reduce(first[:, 0:T], work, AX.X, ALU.max))
            own.link(nc.vector.tensor_tensor(hot, over_tiles(rev), over_experts(first[:, 0:T]), ALU.is_equal))
            nc.vector.tensor_reduce(row_count[:, 0:E], hot.rearrange("p t e -> p e t"), AX.X, ALU.add).then_inc(counted, 1)
            src = hot
            for k, s in enumerate((1, 2, 4, 8, 16, 32)):
                dst = (tally_a, tally_b)[k % 2]
                nc.vector.tensor_copy(dst[:, 0:s, :], src[:, 0:s, :])
                own.link(nc.vector.tensor_tensor(dst[:, s:T, :], src[:, s:T, :], src[:, 0:T - s, :], ALU.add))
                src = dst
            tally = src
            dve.wait_ge(ranked, 1)
            own.link(nc.vector.tensor_copy(slot_f[:, 0:E], second_bank[0][:, E:2 * E]))
            exceeds = work.rearrange("p t e -> p (t e)").rearrange("p (e t) -> p e t", e=E)
            own.link(nc.vector.tensor_tensor(exceeds, slot_f[:, 0:E].unsqueeze(2).to_broadcast([P, E, T]),
                                             steps128.unsqueeze(1).to_broadcast([P, E, T]), ALU.is_gt))
            own.link(nc.vector.tensor_reduce(n_tiles[:, 0:E], exceeds, AX.X, ALU.add))
            src = n_tiles
            for k, s in enumerate((1, 2, 4, 8)):
                dst = (ends_a, ends_b)[k % 2]
                nc.vector.tensor_copy(dst[:, 0:s], src[:, 0:s])
                own.link(nc.vector.tensor_tensor(dst[:, s:E], src[:, s:E], src[:, 0:E - s], ALU.add))
                src = dst
            ends = src
            own.link(nc.vector.tensor_tensor(base[:, 0:E], ends[:, 0:E], n_tiles[:, 0:E], ALU.subtract))
            own.link(nc.vector.tensor_scalar(base[:, 0:E], base[:, 0:E], float(P), -1.0, ALU.mult, ALU.add))
            own.link(nc.vector.tensor_tensor(base[:, 0:E], second_bank[0][:, 0:E], base[:, 0:E], ALU.add))
            own.link(nc.vector.tensor_tensor(work, tally, over_tiles(base[:, 0:E]), ALU.add))
            own.link(nc.vector.tensor_tensor(work, work, hot, ALU.mult))
            own.link(nc.vector.tensor_reduce(slot_f[:, 0:T], work, AX.X, ALU.add))
            nc.vector.tensor_copy(slot[:, :], slot_f[:, 0:T])
            own.link(nc.vector.tensor_tensor(compare, tile_no.unsqueeze(2).to_broadcast([P, SORTED, E]),
                                             ends[:, 0:E].unsqueeze(1).to_broadcast([P, SORTED, E]), ALU.is_ge))
            own.link(nc.vector.tensor_reduce(ends_a[:, 0:SORTED] if ends is ends_b else ends_b[:, 0:SORTED], compare, AX.X, ALU.add))
            which = ends_a if ends is ends_b else ends_b
            nc.vector.tensor_scalar(expert_of[:, 2:2 + SORTED], which[:, 0:SORTED], float(E - 1), None, ALU.min)
            dve.wait_ge(exp_top_done, 1)
            own.link(nc.vector.tensor_scalar(score[:, 0:T], score[:, 0:T], 1.0, None, ALU.add))
            own.link(nc.vector.reciprocal(score[:, 0:T], score[:, 0:T]))
            own.link(nc.vector.tensor_tensor(send_scale[:, :], score[:, 0:T], rstd[:, :], ALU.mult))
            nc.vector.scalar_tensor_tensor(send_shift[:, :], mean[:, :], -1.0, send_scale[:, :], ALU.mult, ALU.mult).then_inc(routed, 1)
            take_v(0, 0, plain)
            take_v(0, 1, plain)

            def take_first(n, j, step):
                width = Q_ITEM[j % 2][2]
                step.wait(dve, first_out, ITEMS * n + j + 1, 2 * ITEMS)
                nc.vector.tensor_reduce(neg_max[:, j % 2, 2 * (j // 2):2 * (j // 2) + 2],
                                        first_bank[j % 2][:, :].rearrange("p (u w) -> p u w", u=2)[:, :, 0:width],
                                        AX.X, ALU.max, negate=True).then_inc(max_taken, 1)

            def split_max(n, step):
                step.wait(dve, max_taken, ITEMS * (n + 1), 2 * ITEMS)
                if n >= 1:
                    b, _ = shared("max", n - 1, 0, step)
                    step.wait(dve, shared_out[b], SHARED[("max", n - 1, 0)] // 2 + 1, SHARED_PER_PAIR // 2)
                own.link(nc.vector.tensor_copy(max_parts[:, :, 0, :], neg_max[:, :, :]))
                own.link(nc.vector.tensor_tensor(neg_max[:, :, :], neg_max[:, :, :], max_parts[:, :, 0, :], ALU.subtract))
                own.link(nc.vector.tensor_copy(max_parts[:, :, 1, :], neg_max[:, :, :]))
                nc.vector.tensor_tensor(max_parts[:, :, 2, :], neg_max[:, :, :], max_parts[:, :, 1, :],
                                        ALU.subtract).then_inc(max_split, 1)

            def normalise(n, qt, step):
                b = shared_wait_out(dve, "turn", n, qt, step)
                heads = shared_bank[b][:, :].rearrange("p (h r) -> p h r", r=32)
                nc.vector.reciprocal(recip[:, qt, :], heads[:, :, DH]).then_inc(recip_done, 1)
                step.wait(dve, recip_done, 2 * n + qt + 1, 4)
                if n >= 1:
                    bb, _ = shared("back", n - 1, qt, step)
                    step.wait(dve, shared_out[bb], SHARED[("back", n - 1, qt)] // 2 + 1, SHARED_PER_PAIR // 2)
                nc.vector.tensor_tensor(att_n[:, qt, :].rearrange("p (h d) -> p h d", d=DH), heads[:, :, 0:DH],
                                        recip[:, qt, :].unsqueeze(2).to_broadcast([P, HEADS, DH]), ALU.mult).then_inc(shared_used[b], 1)

            def add_rest(n, qt, step):
                b = shared_wait_out(dve, "sum", n, qt, step)
                if n % 2 == 0 and qt == 0:
                    step.wait(dve, send_made, n // 2 + 1, 1)
                t = 2 * n + qt
                at = x_res[:, t, :] if step.ahead is None else x_res[:, bass.ds(step.ahead * PT + t, 1), :].rearrange("p a d -> p (a d)")
                nc.vector.tensor_tensor(at, shared_bank[b][:, 0:D], at, ALU.add).then_inc(shared_used[b], 1)

            def gate(i, f, step):
                bg = shared_wait_out(dve, "gate", i, f, step)
                step.wait(dve, tanh_done, 2 * i + f + 1, 2)
                nc.vector.scalar_tensor_tensor(gated[:, :], th[:, :], 1.0, shared_bank[bg][:, :], ALU.add, ALU.mult).then_inc(shared_used[bg], 1)
                shared_wait_used(dve, "gate", i, f, step)
                bu = shared_wait_out(dve, "up", i, f, step)
                assert i == 0 or SHARED[("up", i, 0)] == SHARED[("sum", 2 * i - 1, 1)] + 2
                nc.vector.scalar_tensor_tensor(hT[:, f, :], gated[:, :], 0.5, shared_bank[bu][:, :], ALU.mult, ALU.mult).then_inc(shared_used[bu], 1)

            def batch(n, i, step, items=True):
                for j in range(ITEMS):
                    if items and n + 1 < BATCHES:
                        take_first(n + 1, j, step)
                    if n >= 1 and j in (2, 4):
                        normalise(n - 1, (j - 2) // 2, step)
                    if n >= 1 and j in (10, 11):
                        add_rest(n - 1, j - 10, step)
                    if items and n % 2 == 0 and j in (13, 15):
                        gate(i, (j - 13) // 2, step)
                    if items and n % 2 == 1 and i + 1 < PAIRS and j in (14, 15):
                        take_v(i + 1, j - 14, step)
                if items and n + 1 < BATCHES:
                    split_max(n + 1, step)

            for j in range(ITEMS):
                take_first(0, j, plain)
            split_max(0, plain)

            def pair(i, step):
                batch(2 * i, i, step)
                batch(2 * i + 1, i, step)

            over_pairs(dve, pair, own, 4 * 3)
            batch(BATCHES, PAIRS, plain, items=False)

            def expert_tile(s, ahead):
                wait_count(dve, e_tanh_done, s + 1, ahead)
                wait_count(dve, h_done, s - 1, ahead)
                nc.vector.scalar_tensor_tensor(e_gated[:, s % 2, :], e_th[:, s % 2, :], 1.0, first_bank[s % 2][:, 0:F], ALU.add, ALU.mult).then_inc(e_gated_done, 1)
                wait_count(dve, e_gated_done, s + 1, ahead)
                wait_count(dve, h_turned, s - 1, ahead)
                nc.vector.tensor_tensor(e_h[:, s % 2, :], first_bank[s % 2][:, F:2 * F], e_gated[:, s % 2, :], ALU.mult).then_inc(h_done, 1)

                def take_y(s):
                    wait_count(dve, y_out, s + 1, ahead)
                    if ahead is not None or s >= 4:
                        dve.wait_ge(y_sent[s % 4], plus(s // 4 * 16, ahead, 4))
                    nc.vector.tensor_copy(e_y[:, s % 4, :], shared_bank[s % 2][:, 0:D]).then_inc(y_done, 1)

                if s >= 2:
                    take_y(s - 2)
                if s == SORTED - 1:
                    take_y(s - 1)
                    take_y(s)

            over_sorted(dve, expert_tile)

            dve.wait_ge(bo_added, PAIRS)

            def add_back(c, ahead):
                if ahead is None:
                    dve.wait_ge(back_loaded[c % 4], 16 * (c // 4 + 1))
                    at = x_res[:, c * PT:c * PT + PT, :]
                else:
                    dve.wait_ge(back_loaded[c % 4], ahead * 4 + 16 * (c // 4 + 1))
                    at = x_res[:, bass.ds(ahead * PT + c * PT, PT), :]
                nc.vector.tensor_tensor(at, at, fetched[:, c % 4, :, :], ALU.add).then_inc(all_added, 1)

            with dve.Fori(0, PAIRS // 4) as turn:
                for c in range(4):
                    add_back(c, turn * 4)


def constants():
    p = np.arange(P)
    rev = np.broadcast_to(EXPERTS - np.arange(EXPERTS), (P, EXPERTS))
    steps128 = np.broadcast_to(P * np.arange(TILES), (P, TILES))
    tile_no = np.broadcast_to(np.arange(SORTED), (P, SORTED))
    cst = np.concatenate([np.eye(P), p[:, None] < p[None, :], rev, steps128, tile_no], 1).astype(np.float32)
    mask_q, mask_k = np.zeros((P, SEQ), np.float32), np.zeros((P, SEQ), np.float32)
    pos = np.arange(SEQ)
    blk, off = pos // WINDOW, pos % WINDOW
    for r, row in enumerate(FINE_ROWS):
        parity, key = r // WINDOW, r % WINDOW
        allowed = np.where(blk % 2 == parity, key <= off, key > off)
        mask_q[row] = np.where(allowed, 0.0, FAR)
        mask_k[row] = (blk % 2 == parity) & (off == key)
    for b, row in enumerate(BLOCK_ROWS):
        mask_q[row] = np.where((b == blk) | (b == blk - 1), 0.0, FAR)
        mask_k[row] = blk == b
    mask_k[MAX_ROW:MAX_ROW + 3] = 1.0
    tok = (np.arange(TILES)[None, :] * P + p[:, None]).astype(np.int32)
    mask_q, mask_k = ((m.view(np.uint32) >> 16).astype(np.uint16) for m in (mask_q, mask_k))
    return cst, mask_q, mask_k, tok


def kernel(**inputs):
    import concourse.bacc as _bacc
    from concourse.bass_utils import run_bass_kernel_spmd as _run

    g = {k.removeprefix("L0_"): np.asarray(v) for k, v in inputs.items()}

    def by_dim_then_head(w):
        return w.reshape(HEADS, DH, -1).swapaxes(0, 1).reshape(D, -1)

    cst, mask_q, mask_k, tok = constants()
    arrays = {
        "x": g["attn_x"].reshape(TOKENS, D),
        "wq": by_dim_then_head(g["attn_Wq"]).T, "bq": by_dim_then_head(g["attn_bq"]),
        "wk": by_dim_then_head(g["attn_Wk"]).T, "bk": by_dim_then_head(g["attn_bk"]),
        "wv": g["attn_Wv"].T, "bv": g["attn_bv"].reshape(1, D),
        "wo": g["attn_Wo"].T, "bo": g["attn_bo"].reshape(1, D),
        "wr": g["ffn_w_router"].T, "wgu": g["ffn_gate_up_proj"], "wdn": g["ffn_down_proj"],
        "wg": g["ffn_w_gate"].T, "wu": g["ffn_w_up"].T, "wd": g["ffn_w_down"].T,
        "cst": cst, "mask_q": mask_q, "mask_k": mask_k, "tok": tok,
    }
    nc = _bacc.Bacc("TRN2", target_bir_lowering=False, num_devices=1)
    args, given = [], {}
    for name, a in arrays.items():
        given[f"in_{name}"] = a = np.ascontiguousarray(a)
        args.append(nc.dram_tensor(f"in_{name}", list(a.shape), mybir.dt.from_np(a.dtype), kind="ExternalInput").ap())
    out = nc.dram_tensor("out_0", [TOKENS, D], F32, kind="ExternalOutput").ap()
    build(nc, *args, out)
    r = _run(nc, [given], core_ids=[0])
    return r.results[0]["out_0"].reshape(BATCHES, SEQ, D)
```

```python
from contextlib import ExitStack

import concourse.bass as bass
import numpy as np
from concourse import mybir

F32, BF16 = mybir.dt.float32, mybir.dt.bfloat16
I32, U32, U16 = mybir.dt.int32, mybir.dt.uint32, mybir.dt.uint16
ALU = mybir.AluOpType
ACT = mybir.ActivationFunctionType
AX = mybir.AxisListType

P = 128
BATCHES, SEQ, D = 32, 256, 128
HEADS, DH, WINDOW = 16, 8, 32
EXPERTS, F = 16, 256
GROUPS = HEADS // 2
TOKENS = BATCHES * SEQ
TILES = TOKENS // P
PAIR = 2 * SEQ
PAIRS = TOKENS // PAIR
PT = PAIR // P
SORTED = TILES + EXPERTS
EPS = 1e-5
FAR = -float(2.0**100)
ROW = D + 4

PART_ROWS = [0, 8, 16, 64, 72, 80]
Q_PARTS = [0, 0, 1, 1, 0, 2]
K_PARTS = [0, 1, 0, 1, 2, 0]
FINE_ROWS = list(range(24, 64)) + list(range(88, 112))
BLOCK_ROWS = list(range(112, 120))
MAX_ROW = 120
ROWS_Q, ROWS_K = 120, 123
MASK_ROWS = [slice(24, 64), slice(88, 123)]

Q_ITEM = [(0, 0, 128), (128, 96, 160)]
K_ITEM = [(0, 0, 160), (128, 128, 128)]
ITEMS = 16
LEAD = 6
POST = {3: "turn", 6: "back", 8: "sum", 11: "max"}
EVEN = {1: ("v", 0), 5: ("v", 1), 10: ("q", 0), 13: ("k", 0)}
ODD = {0: ("gate", 0), 1: ("up", 0), 9: ("gate", 1), 13: ("up", 1)}


def shared_uses_after(n, j):
    uses, i = [], n // 2
    if j in POST:
        of = n + 1 if POST[j] == "max" else n - 1
        if 0 <= of < BATCHES:
            uses.append((POST[j], of, 0))
    for when in (EVEN, ODD)[n % 2].items():
        if when[0] == j:
            what, part = when[1]
            of = i + 2 if what in "qk" else i + 1
            if of < PAIRS:
                uses.append((what, of, part))
    return uses


def shared_bank_order():
    order = [("q", 0, 0), ("k", 0, 0), ("q", 1, 0), ("k", 1, 0), ("max", 0, 0), ("v", 0, 0), ("v", 0, 1)]
    order += [("gate", 0, 0), ("up", 0, 0), ("gate", 0, 1), ("up", 0, 1)]
    for n in range(BATCHES):
        for j in range(ITEMS):
            order += shared_uses_after(n, j)
    order += [(what, BATCHES - 1, 0) for what in ("turn", "back", "sum")]
    return {use: at for at, use in enumerate(order)}


SHARED = shared_bank_order()
SHARED_PER_PAIR = 16


class Step:

    def __init__(self, ahead=None):
        self.ahead = ahead

    def value(self, at_ref, per_pair):
        return at_ref if self.ahead is None else at_ref + self.ahead * per_pair

    def wait(self, eng, sem, at_ref, per_pair):
        if self.ahead is not None or at_ref > 0:
            eng.wait_ge(sem, self.value(at_ref, per_pair))


class Count:

    def __init__(self, eng, sem):
        self.eng, self.sem, self.n, self.extra = eng, sem, 0, None

    def link(self, ins):
        ins.then_inc(self.sem, 1)
        self.n += 1
        self.eng.wait_ge(self.sem, self.n if self.extra is None else self.extra + self.n)

    def enter(self, turn, per_turn):
        self.extra, self.start, self.per_turn = turn * per_turn, self.n, per_turn

    def leave(self, turns):
        assert self.n - self.start == self.per_turn, (self.n - self.start, self.per_turn)
        self.n, self.extra = self.start + turns * self.per_turn, None


def build(nc, x, wq, bq, wk, bk, wv, bv, wo, bo, wr, wgu, wdn, wg, wu, wd, cst, mask_q, mask_k, tok, out):
    ctx = ExitStack()
    with ctx:
        def sb(name, shape, dt=F32):
            return ctx.enter_context(nc.sbuf_tensor(name, shape, dt))

        def sem(name):
            return ctx.enter_context(nc.semaphore(name))

        xnT_dram = nc.dram_tensor("xnT_keep", [PAIRS, P, PAIR], F32).ap()
        sorted_dram = nc.dram_tensor("sorted_keep", [SORTED * P, ROW], F32).ap()
        back_dram = nc.dram_tensor("back_keep", [TOKENS, D], F32).ap()

        x_res = sb("x_res", [P, TILES, D])
        stack = [sb(f"stack{b}", [P, HEADS, 2, PAIR], BF16) for b in range(2)]
        gu_sb = sb("gu_sb", [P, EXPERTS * 2 * F])
        dn_sb = sb("dn_sb", [P, EXPERTS * 2 * D])
        v_sb = [sb(f"v_sb{b}", [P, PT, GROUPS, 2, 2 * (DH + 1)]) for b in range(2)]
        xnT = [sb(f"xnT{b}", [P, PAIR]) for b in range(2)]
        q32 = sb("q32", [P, PAIR])
        k32 = sb("k32", [P, PAIR])
        parts = sb("parts", [P, 6, PAIR], BF16)
        probs = sb("probs", [P, 4, 2, 160])
        att = sb("att", [P, 2, SEQ])
        att_n = sb("att_n", [P, 2, D])
        att_nT = sb("att_nT", [P, 2, P])
        recip = sb("recip", [P, 2 * GROUPS, 2])
        neg_max = sb("neg_max", [P, 2, 2, HEADS])
        max_parts = sb("max_parts", [P, 2, 3, HEADS], BF16)
        maxT = sb("maxT", [3 * HEADS, SEQ], BF16)
        th = sb("th", [P, PAIR])
        gated = sb("gated", [P, PAIR])
        hT = sb("hT", [P, 2, 2, PAIR])
        wq_sb, wk_sb, wv_sb, wo_sb = (sb(n, [P, D]) for n in ("wq_sb", "wk_sb", "wv_sb", "wo_sb"))
        wr_sb = sb("wr_sb", [P, EXPERTS])
        wg_sb, wu_sb, wd_sb = (sb(n, [P, F]) for n in ("wg_sb", "wu_sb", "wd_sb"))
        bq_sb, bk_sb, bqs = (sb(n, [P, 1]) for n in ("bq_sb", "bk_sb", "bqs"))
        bv_sb, bo_sb = sb("bv_sb", [P, D]), sb("bo_sb", [P, D])
        cst_sb = sb("cst_sb", [P, cst.shape[1]])
        ident, before = cst_sb[:, 0:P], cst_sb[:, P:2 * P]
        rev = cst_sb[:, 2 * P:2 * P + EXPERTS]
        steps128 = cst_sb[:, 2 * P + EXPERTS:2 * P + EXPERTS + TILES]
        tile_no = cst_sb[:, 2 * P + EXPERTS + TILES:2 * P + EXPERTS + TILES + SORTED]
        ident_bf = sb("ident_bf", [P, P], BF16)
        mask_q_sb, mask_k_sb = sb("mask_q_sb", [P, PAIR], BF16), sb("mask_k_sb", [P, PAIR], BF16)
        tok_sb = sb("tok_sb", [P, TILES], I32)
        ones = sb("ones", [P, P])
        stats = sb("stats", [P, 2, PT, 6])
        moments = sb("moments", [P, 4, PT, 2])
        var_eps = sb("var_eps", [P, PT])
        neg_half = sb("neg_half", [P, PT])
        mean, rstd = sb("mean", [P, TILES]), sb("rstd", [P, TILES])
        slot = sb("slot", [P, TILES], I32)
        send_scale, send_shift = sb("send_scale", [P, TILES]), sb("send_shift", [P, TILES])
        send = sb("send", [P, 2, PT, ROW])
        expert_of = sb("expert_of", [P, SORTED + 4], I32)

        def scratch(at, *shape):
            n = int(np.prod(shape))
            ap = gu_sb[:, at:at + n]
            return ap if len(shape) == 1 else ap.rearrange("p (a b) -> p a b", b=shape[1])

        E, T = EXPERTS, TILES
        xn = [scratch(b * PAIR, PT, D) for b in range(2)]
        logits = scratch(1024, T, E)
        hot, tally_a, tally_b, work = (scratch(2048 + 1024 * k, T, E) for k in range(4))
        compare = scratch(6144, SORTED, E)
        small = [scratch(7424 + 80 * k, 80) for k in range(9)]
        top, first, score, row_count, n_tiles, ends_a, ends_b, base, slot_f = small
        late, late2 = (stack[b][:, :, :, :].rearrange("p h c n -> p (h c n)").bitcast(F32) for b in range(2))
        ring = late[:, 0:8 * ROW].rearrange("p (r c) -> p r c", c=ROW)
        rowT = late[:, 1100:1100 + 2 * P].rearrange("p (r c) -> p r c", c=P)
        e_th = late[:, 1400:1400 + 2 * F].rearrange("p (r c) -> p r c", c=F)
        e_gated = late2[:, 2100:2100 + 2 * F].rearrange("p (r c) -> p r c", c=F)
        e_h = late[:, 2300:2300 + 2 * F].rearrange("p (r c) -> p r c", c=F)
        e_hT = late[:, 2900:2900 + 2 * F].rearrange("p (r c) -> p r c", c=F)
        e_y = late[:, 3500:3500 + 4 * D].rearrange("p (r c) -> p r c", c=D)
        fetched = late2[:, 0:4 * PT * D].rearrange("p (r t d) -> p r t d", r=4, d=D)

        bank = [ctx.enter_context(nc.psum_tensor(f"bank{b}", [P, 512], F32)) for b in range(8)]
        first_bank, second_bank, att_bank, shared_bank = bank[0:2], bank[2:4], bank[4:6], bank[6:8]

        x_loaded = [sem(f"x_loaded{b}") for b in range(2)]
        const_loaded, weights_loaded = sem("const_loaded"), sem("weights_loaded")
        masks_loaded, stacks_masked = sem("masks_loaded"), sem("stacks_masked")
        blank_made, blanks_stored = sem("blank_made"), sem("blanks_stored")
        prepared, waits_passed = sem("prepared"), sem("waits_passed")
        stats_done, moments_done, rstd_done = sem("stats_done"), sem("moments_done"), sem("rstd_done")
        xn_done, xn_turned, xnT_done = sem("xn_done"), sem("xn_turned"), sem("xnT_done")
        xnT_stored = [sem(f"xnT_stored{b}") for b in range(2)]
        logits_out, logits_done = sem("logits_out"), sem("logits_done")
        top_done, exp_top_done, counted, ranked, routed = (
            sem(n) for n in ("top_done", "exp_top_done", "counted", "ranked", "routed"))
        dve_own, pool_own = sem("dve_own"), sem("pool_own")
        send_made = sem("send_made")
        sent = [sem(f"sent{b}") for b in range(2)]
        experts_loaded = sem("experts_loaded")
        xnT_loaded = [sem(f"xnT_loaded{b}") for b in range(2)]
        parts_made = sem("parts_made")
        stack_loaded = [sem(f"stack_loaded{b}") for b in range(2)]
        first_out, max_taken = sem("first_out"), sem("max_taken")
        second_out, exp_done, att_added, att_taken = (
            sem(n) for n in ("second_out", "exp_done", "att_added", "att_taken"))
        shared_out = [sem(f"shared_out{b}") for b in range(2)]
        shared_used = [sem(f"shared_used{b}") for b in range(2)]
        max_split, max_loaded = sem("max_split"), sem("max_loaded")
        recip_done, tanh_done, bo_added = sem("recip_done"), sem("tanh_done"), sem("bo_added")
        row_loaded = [sem(f"row_loaded{r}") for r in range(8)]
        row_turned, rowT_done, gu_out, e_tanh_done, e_gated_done, h_done = (
            sem(n) for n in ("row_turned", "rowT_done", "gu_out", "e_tanh_done", "e_gated_done", "h_done"))
        h_turned, e_hT_done, y_out, y_done = (sem(n) for n in ("h_turned", "e_hT_done", "y_out", "y_done"))
        y_sent = [sem(f"y_sent{r}") for r in range(4)]
        back_loaded = [sem(f"back_loaded{r}") for r in range(4)]
        all_added, out_stored = sem("all_added"), sem("out_stored")

        block = ctx.enter_context(nc.Block())

        x_by_chunk = x.rearrange("(c k p) d -> c p k d", p=P, k=PT)
        out_by_chunk = out.rearrange("(c k p) d -> c p k d", p=P, k=PT)
        back_by_chunk = back_dram.rearrange("(c k p) d -> c p k d", p=P, k=PT)

        def wait_last(eng, sems, uses, step):
            last = {}
            for use in uses:
                if use in SHARED:
                    b = SHARED[use] % 2
                    last[b] = max(last.get(b, 0), SHARED[use] // 2 + 1)
            for b, at in last.items():
                step.wait(eng, sems[b], at, SHARED_PER_PAIR // 2)

        def shared_wait_out(eng, uses, step):
            wait_last(eng, shared_out, uses, step)
            return SHARED[uses[0]] % 2

        def shared_wait_used(eng, uses, step):
            wait_last(eng, shared_used, uses, step)

        def shared_open(pe, use, step, after=()):
            at = SHARED[use]
            assert all(SHARED[a] < at for a in after)
            before = [a for a, k in SHARED.items() if k == at - 2]
            wait_last(pe, shared_used, [*before, *after], step)
            return at % 2

        def over_pairs(eng, emit, count=None, per_turn=0):
            for i in (0, 1):
                emit(i, Step())
            with eng.Fori(0, 6) as turn:
                if count:
                    count.enter(turn, per_turn)
                for i in (2, 3):
                    emit(i, Step(turn * 2))
            if count:
                count.leave(6)
            for i in (14, 15):
                emit(i, Step())

        def over_sorted(eng, emit):
            for s in range(8):
                emit(s, None)
            with eng.Fori(0, SORTED // 8 - 2) as turn:
                for s in range(8, 16):
                    emit(s, turn * 8)
            for s in range(SORTED - 8, SORTED):
                emit(s, None)

        def pass_wait(eng):
            eng.sem_inc(waits_passed, 1)

        def plus(value, ahead, factor=1):
            return value if ahead is None else value + (ahead if factor == 1 else ahead * factor)

        def wait_count(eng, s, value, ahead):
            if ahead is not None or value > 0:
                eng.wait_ge(s, plus(value, ahead))

        @block.sync
        def _(sp):
            def load_x(c, half, b, to):
                if to is None or to > 0:
                    sp.wait_ge(x_loaded[b], half)
                    pass_wait(sp)
                sp.dma_start(x_res[:, bass.ds(c * PT, PT), :] if to is None else x_res[:, c * PT:c * PT + PT, :],
                             x_by_chunk[bass.ds(c, 1), :, :, :].rearrange("a p k d -> (a p) k d") if to is None else x_by_chunk[c]).then_inc(x_loaded[b], 16)

            for c in (0, 1):
                load_x(c, 0, c, 0)
            with sp.Fori(1, PAIRS // 2) as k:
                for b in range(2):
                    load_x(k * 2 + b, k * 16, b, None)
            sp.wait_ge(masks_loaded, 32)
            for b in range(2):
                for c, mask in enumerate((mask_q_sb, mask_k_sb)):
                    for rows in MASK_ROWS:
                        sp.dma_start(stack[b][rows, :, c, :],
                                     mask[rows, :].unsqueeze(1).to_broadcast([rows.stop - rows.start, HEADS, PAIR])).then_inc(stacks_masked, 16)

            def load_xnT(i, step):
                if i >= 2:
                    shared_wait_out(sp, [("up", i - 2, 1)], step)
                    pass_wait(sp)
                src = xnT_dram[i] if step.ahead is None else xnT_dram[bass.ds(step.ahead + i, 1), :, :].rearrange("a p n -> (a p) n")
                sp.dma_start(xnT[i % 2][:, :], src).then_inc(xnT_loaded[i % 2], 16)

            def stack_parts(i, step):
                step.wait(sp, parts_made, 2 * i + 2, 2)
                pass_wait(sp)
                step.wait(sp, second_out, 2 * ITEMS * (i - 1), 2 * ITEMS)
                pass_wait(sp)
                for row, q_part, k_part in zip(PART_ROWS, Q_PARTS, K_PARTS):
                    both = parts[:, q_part:3 + k_part + 1:3 + k_part - q_part, :]
                    sp.dma_start(stack[i % 2][row:row + DH, :, :, :].rearrange("p h c n -> p (h c n)"), both).then_inc(stack_loaded[i % 2], 16)

            def stack_max(n, step):
                shared_wait_used(sp, [("max", n, 0)], step)
                half = (n % 2) * SEQ
                sp.dma_start(stack[(n // 2) % 2][MAX_ROW:MAX_ROW + 3, :, 0, half:half + SEQ], maxT[:, :]).then_inc(max_loaded, 16)

            for b in range(2):
                sp.wait_ge(xnT_stored[b], 16 * (PAIRS // 2))
            sp.wait_ge(stacks_masked, 64 * len(MASK_ROWS))
            sp.wait_ge(logits_out, PAIRS)
            plain = Step()
            load_xnT(0, plain)
            load_xnT(1, plain)
            stack_parts(0, plain)
            stack_parts(1, plain)
            sp.wait_ge(routed, 1)
            sp.dma_start(gu_sb[:, :].rearrange("p (e f) -> p e f", e=EXPERTS), wgu.rearrange("e p f -> p e f")).then_inc(experts_loaded, 16)
            sp.dma_start(dn_sb[:, :].rearrange("p (e u d) -> p e u d", e=EXPERTS, u=2), wdn.rearrange("e (u p) d -> p e u d", p=P)).then_inc(experts_loaded, 16)
            stack_max(0, plain)

            def pair(i, step):
                if 1 <= i < PAIRS - 1:
                    stack_parts(i + 1, step)
                if i + 2 < PAIRS:
                    load_xnT(i + 2, step)
                stack_max(2 * i + 1, step)
                if i + 1 < PAIRS:
                    stack_max(2 * i + 2, step)

            over_pairs(sp, pair)

            sp.wait_ge(att_added, ITEMS * BATCHES)
            for b in range(2):
                sp.wait_ge(sent[b], 16 * TILES // 2)
            by_tile = sorted_dram.rearrange("(s p) c -> s p c", p=P)

            def load_row(s, ahead):
                if ahead is not None or s >= 8:
                    sp.wait_ge(y_sent[s % 4], plus((s - 8) // 4 * 16 + 16, ahead, 4))
                    pass_wait(sp)
                src = by_tile[s] if ahead is None else by_tile[bass.ds(ahead + s, 1), :, :].rearrange("a p c -> (a p) c")
                sp.dma_start(ring[:, s % 8, :], src).then_inc(row_loaded[s % 8], 16)

            over_sorted(sp, load_row)

            for r in range(4):
                sp.wait_ge(y_sent[r], 16 * SORTED // 4)

            def load_back(c, ahead):
                if ahead is not None:
                    sp.wait_ge(all_added, plus(c - 3, ahead))
                    pass_wait(sp)
                src = back_by_chunk[c] if ahead is None else back_by_chunk[bass.ds(ahead + c, 1), :, :, :].rearrange("a p k d -> (a p) k d")
                sp.dma_start(fetched[:, c % 4, :, :], src).then_inc(back_loaded[c % 4], 16)

            for c in range(4):
                load_back(c, None)
            with sp.Fori(0, PAIRS // 4 - 1) as turn:
                for c in range(4, 8):
                    load_back(c, turn * 4)
            sp.wait_ge(out_stored, 16 * PAIRS)

        @block.gpsimd
        def _(pool):
            own = Count(pool, pool_own)
            blank = send[:, 0:2, :, :].rearrange("p a b c -> p (a b) c")
            nc.gpsimd.memset(blank[:, :, 0:D], 0.0)
            nc.gpsimd.memset(blank[:, :, D:ROW].bitcast(I32), TOKENS).then_inc(blank_made, 1)
            own.link(nc.gpsimd.memset(neg_half[:, :], -0.5))
            for c in range(PAIRS):
                t = slice(c * PT, c * PT + PT)
                pool.wait_ge(moments_done, c + 1)
                if c >= 1:
                    pool.wait_ge(rstd_done, c)
                own.link(nc.gpsimd.tensor_scalar(var_eps[:, :], moments[:, c % 4, :, 1], 1.0, EPS, ALU.mult, ALU.add))
                nc.gpsimd.tensor_copy(mean[:, t], moments[:, c % 4, :, 0])
                nc.gpsimd.tensor_tensor(rstd[:, t], var_eps[:, :], neg_half[:, :], ALU.pow).then_inc(rstd_done, 1)

            plain = Step()

            def split(i):
                for k, full in enumerate((q32, k32)):
                    shared_wait_used(pool, [("qk"[k], i, 0)], plain)
                    own.link(nc.gpsimd.tensor_tensor(full[:, :], full[:, :], parts[:, 3 * k, :], ALU.subtract))
                    own.link(nc.gpsimd.tensor_scalar(parts[:, 3 * k + 1, :], full[:, :], 1.0, 0.0, ALU.mult, ALU.add))
                    nc.gpsimd.tensor_tensor(parts[:, 3 * k + 2, :], full[:, :], parts[:, 3 * k + 1, :], ALU.subtract).then_inc(parts_made, 1)

            def scatter(g):
                b = g % 2
                if g == 0:
                    pool.wait_ge(blanks_stored, 16 * (SORTED // 8))
                    pool.wait_ge(routed, 1)
                    for k in range(2):
                        pool.wait_ge(x_loaded[k], 16 * (PAIRS // 2))
                if g >= 2:
                    pool.wait_ge(sent[b], 16 * PT * (g // 2))
                for k in range(PT):
                    t = g * PT + k
                    nc.gpsimd.tensor_scalar(send[:, b, k, 0:D], x_res[:, t, :], send_scale[:, t:t + 1],
                                            send_shift[:, t:t + 1], ALU.mult, ALU.add)
                nc.gpsimd.tensor_copy(send[:, b, :, D:D + 1].bitcast(I32),
                                      tok_sb[:, g * PT:g * PT + PT].unsqueeze(2)).then_inc(send_made, 1)
                pool.wait_ge(send_made, g + 1)
                for k in range(PT):
                    t = g * PT + k
                    nc.gpsimd.indirect_dma_start(
                        sorted_dram, bass.IndirectOffsetOnAxis(slot[:, t:t + 1].bitcast(U32), 0),
                        send[:, b, k, :], None, bounds_check=SORTED * P - 1, oob_is_err=False).then_inc(sent[b], 16)

            def add_bo(i):
                shared_wait_used(pool, [("sum", 2 * i, 0), ("sum", 2 * i + 1, 0)], plain)
                t = slice(i * PT, i * PT + PT)
                nc.gpsimd.tensor_tensor(x_res[:, t, :], x_res[:, t, :], bo_sb[:, :].unsqueeze(1).to_broadcast([P, PT, D]),
                                        ALU.add).then_inc(bo_added, 1)

            split(0)
            split(1)
            for i in range(PAIRS):
                scatter(i)
                if i >= 1:
                    add_bo(i - 1)
                if i + 2 < PAIRS:
                    split(i + 2)
            add_bo(PAIRS - 1)

            def send_back(s, ahead):
                pool.wait_ge(y_done, plus(s + 1, ahead))
                pass_wait(pool)
                nc.gpsimd.indirect_dma_start(
                    back_dram, bass.IndirectOffsetOnAxis(ring[:, s % 8, D:D + 1].bitcast(U32), 0),
                    e_y[:, s % 4, :], None, bounds_check=TOKENS - 1, oob_is_err=False).then_inc(y_sent[s % 4], 16)

            over_sorted(pool, send_back)

        @block.scalar
        def _(act):
            act.dma_start(cst_sb[:, :], cst).then_inc(const_loaded, 16)
            act.dma_start(wr_sb[:, :], wr).then_inc(const_loaded, 16)
            act.dma_start(mask_q_sb[:, :].bitcast(U16), mask_q).then_inc(masks_loaded, 16)
            act.dma_start(mask_k_sb[:, :].bitcast(U16), mask_k).then_inc(masks_loaded, 16)
            loads = [(wq_sb[:, :], wq), (wk_sb[:, :], wk), (wv_sb[:, :], wv), (wo_sb[:, :], wo), (wg_sb[:, :], wg),
                     (wu_sb[:, :], wu), (wd_sb[:, :].rearrange("p (u d) -> p u d", u=2), wd.rearrange("(u p) d -> p u d", p=P)),
                     (bq_sb[:, :], bq), (bk_sb[:, :], bk), (bv_sb[:, :], bv.to_broadcast([P, D])),
                     (bo_sb[:, :], bo.to_broadcast([P, D])), (tok_sb[:, :], tok)]
            for dst, src in loads:
                act.dma_start(dst, src).then_inc(weights_loaded, 16)

            def take_xnT(c, b, half, runtime):
                act.wait_ge(xn_turned, c + 1)
                if runtime:
                    act.wait_ge(logits_out, c - 1)
                    act.wait_ge(xnT_stored[b], half * 16)
                act.activation(xnT[b][:, :], first_bank[b][:, :], ACT.Copy).then_inc(xnT_done, 1)
                act.wait_ge(xnT_done, c + 1)
                dst = xnT_dram[bass.ds(c, 1), :, :].rearrange("a p n -> (a p) n") if runtime else xnT_dram[c]
                act.dma_start(dst, xnT[b][:, :]).then_inc(xnT_stored[b], 16)

            def take_logits(c, b, runtime):
                act.wait_ge(logits_out, c + 1)
                dst = logits[:, bass.ds(c * PT, PT), :] if runtime else logits[:, c * PT:c * PT + PT, :]
                act.activation(dst, second_bank[b][:, 0:PT * E].rearrange("p (t e) -> p t e", e=E), ACT.Copy).then_inc(logits_done, 1)

            take_xnT(0, 0, 0, False)
            take_xnT(1, 1, 0, False)
            take_logits(0, 0, False)
            blank = send[:, 0:2, :, :].rearrange("p a b c -> p (a b) c")
            act.wait_ge(blank_made, 1)
            for k in range(SORTED // 8):
                act.dma_start(sorted_dram[k * 8 * P:(k + 1) * 8 * P, :].rearrange("(p r) c -> p r c", p=P), blank).then_inc(blanks_stored, 16)
            with act.Fori(1, PAIRS // 2) as k:
                take_xnT(k * 2, 0, k, True)
                take_logits(k * 2 - 1, 1, True)
                take_xnT(k * 2 + 1, 1, k, True)
                take_logits(k * 2, 0, True)
            take_logits(PAIRS - 1, 1, False)

            act.wait_ge(top_done, 1)
            act.activation(score[:, 0:T], top[:, 0:T], ACT.Exp, scale=-1.0).then_inc(exp_top_done, 1)

            def take_qk(what, i, step):
                b = shared_wait_out(act, [(what, i, 0)], step)
                if what == "q":
                    step.wait(act, parts_made, 2 * i, 2)
                    if i >= 1:
                        step.wait(act, stack_loaded[(i - 1) % 2], 96 * ((i - 1) // 2 + 1), 48)
                full, part, scale, bias = (q32, 0, DH**-0.5, bqs) if what == "q" else (k32, 3, 1.0, bk_sb)
                act.activation(parts[:, part, :], shared_bank[b][:, :], ACT.Identity, bias=bias[:, :], scale=scale)
                act.activation(full[:, :], shared_bank[b][:, :], ACT.Identity, bias=bias[:, :], scale=scale).then_inc(shared_used[b], 1)

            def take_max(n, step):
                b = shared_wait_out(act, [("max", n, 0)], step)
                step.wait(act, max_loaded, 16 * n, 32)
                act.activation(maxT[:, :], shared_bank[b][0:3 * HEADS, 0:SEQ // 2].bitcast(BF16), ACT.Copy).then_inc(shared_used[b], 1)

            def take_att(n, step):
                step.wait(act, att_added, ITEMS * (n + 1), 2 * ITEMS)
                wait_last(act, shared_out, [("turn", n - 1, 0)], step)
                act.activation(att[:, :, :].rearrange("p s n -> p (s n)"), att_bank[n % 2][:, :],
                               ACT.Copy).then_inc(att_taken, 1)

            def take_back(n, step):
                b = shared_wait_out(act, [("back", n, 0), ("sum", n - 1, 0)], step)
                act.activation(att_nT[:, :, :].rearrange("p q n -> p (q n)"), shared_bank[b][:, 0:SEQ], ACT.Copy).then_inc(shared_used[b], 1)

            def take_gate(i, f, step):
                b = shared_wait_out(act, [("gate", i, f)], step)
                shared_wait_used(act, [("gate", i + f - 1, 1 - f)], step)
                act.activation(th[:, :], shared_bank[b][:, :], ACT.Tanh, scale=0.5).then_inc(tanh_done, 1)

            def batch(n, i, step):
                for j in range(ITEMS):
                    width = K_ITEM[j % 2][2]
                    step.wait(act, second_out, ITEMS * n + j + 1, 2 * ITEMS)
                    step.wait(act, att_added, ITEMS * n + j - 3, 2 * ITEMS)
                    act.activation(probs[:, j % 4, :, 0:width],
                                   second_bank[j % 2][:, :].rearrange("p (u w) -> p u w", u=2)[:, :, 0:width],
                                   ACT.Exp).then_inc(exp_done, 1)
                    if j == 1 and n >= 1:
                        take_att(n - 1, step)
                    if j == 6 and n >= 1:
                        take_back(n - 1, step)
                    if j == 11 and n + 1 < BATCHES:
                        take_max(n + 1, step)
                    if n % 2 == 1 and i + 1 < PAIRS and j in (0, 9):
                        take_gate(i + 1, (0, 9).index(j), step)
                    if n % 2 == 0 and i + 2 < PAIRS and j in (10, 13):
                        take_qk("q" if j == 10 else "k", i + 2, step)

            plain = Step()
            for i in (0, 1):
                take_qk("q", i, plain)
                take_qk("k", i, plain)
            take_max(0, plain)
            take_gate(0, 0, plain)
            take_gate(0, 1, plain)

            def pair(i, step):
                batch(2 * i, i, step)
                batch(2 * i + 1, i, step)

            over_pairs(act, pair)
            take_att(BATCHES - 1, plain)
            take_back(BATCHES - 1, plain)

            def expert_tile(s, ahead):
                def take_row(s):
                    wait_count(act, row_turned, s + 1, ahead)
                    wait_count(act, gu_out, s - 1, ahead)
                    act.activation(rowT[:, s % 2, :], second_bank[s % 2][:, 0:P], ACT.Copy).then_inc(rowT_done, 1)

                if s == 0 and ahead is None:
                    take_row(0)
                if s + 1 < SORTED or ahead is not None:
                    take_row(s + 1)
                wait_count(act, gu_out, s + 1, ahead)
                wait_count(act, e_gated_done, s - 1, ahead)
                act.activation(e_th[:, s % 2, :], first_bank[s % 2][:, 0:F], ACT.Tanh, scale=0.5).then_inc(e_tanh_done, 1)

                def take_h(s):
                    wait_count(act, h_turned, s + 1, ahead)
                    wait_count(act, y_out, s - 1, ahead)
                    act.activation(e_hT[:, s % 2, :], att_bank[s % 2][:, 0:F], ACT.Copy, scale=0.5).then_inc(e_hT_done, 1)

                if s >= 1:
                    take_h(s - 1)
                if s == SORTED - 1:
                    take_h(s)

            over_sorted(act, expert_tile)

            for c in range(PAIRS):
                act.wait_ge(all_added, c + 1)
                act.dma_start(out_by_chunk[c], x_res[:, c * PT:c * PT + PT, :]).then_inc(out_stored, 16)

        @block.tensor
        def _(pe):
            pe.wait_ge(const_loaded, 32)

            def norm_chunk(c, b, runtime):
                pe.wait_ge(xn_done, c + 1)
                if runtime:
                    pe.wait_ge(xnT_done, c - 1)
                for k in range(PT):
                    last = nc.tensor.transpose(first_bank[b][:, k * P:(k + 1) * P], xn[b][:, k, :], ident)
                last.then_inc(xn_turned, 1)
                pe.wait_ge(xnT_done, c + 1)
                if runtime:
                    pe.wait_ge(logits_done, c - 1)
                for k in range(PT):
                    last = nc.tensor.matmul(second_bank[b][:, k * E:(k + 1) * E], xnT[b][:, k * P:(k + 1) * P],
                                            wr_sb[:, :], start=True, stop=True)
                last.then_inc(logits_out, 1)

            norm_chunk(0, 0, False)
            norm_chunk(1, 1, False)
            with pe.Fori(1, PAIRS // 2) as k:
                norm_chunk(k * 2, 0, True)
                norm_chunk(k * 2 + 1, 1, True)

            pe.wait_ge(weights_loaded, 16 * 12)
            pe.wait_ge(prepared, 1)

            def project(what, i, step):
                b = shared_open(pe, (what, i, 0), step)
                step.wait(pe, xnT_loaded[i % 2], 16 * (i // 2 + 1), 8)
                nc.tensor.matmul(shared_bank[b][:, :], (wq_sb if what == "q" else wk_sb)[:, :], xnT[i % 2][:, :],
                                 start=True, stop=True).then_inc(shared_out[b], 1)

            def project_v(i, half, step):
                b = shared_open(pe, ("v", i, half), step)
                for k in (2 * half, 2 * half + 1):
                    last = nc.tensor.matmul(shared_bank[b][:, (k % 2) * D:(k % 2 + 1) * D], xnT[i % 2][:, k * P:(k + 1) * P],
                                            wv_sb[:, :], start=True, stop=True)
                last.then_inc(shared_out[b], 1)

            def gate_up(what, i, f, step):
                b = shared_open(pe, (what, i, f), step)
                w = wg_sb if what == "gate" else wu_sb
                nc.tensor.matmul(shared_bank[b][:, :], w[:, f * P:(f + 1) * P], xnT[i % 2][:, :],
                                 start=True, stop=True).then_inc(shared_out[b], 1)

            def first_scores(n, j, step):
                (q0, k0, width), i = Q_ITEM[j % 2], n // 2
                if j == 0 and n % 2 == 0:
                    step.wait(pe, stack_loaded[i % 2], 96 * (i // 2 + 1), 48)
                step.wait(pe, max_taken, ITEMS * n + j - 1, 2 * ITEMS)
                at = (n % 2) * SEQ
                for u in range(2):
                    h = 2 * (j // 2) + u
                    last = nc.tensor.matmul(first_bank[j % 2][:, u * 256:u * 256 + width],
                                            stack[i % 2][0:ROWS_Q, h, 0, at + q0:at + q0 + P],
                                            stack[i % 2][0:ROWS_Q, h, 1, at + k0:at + k0 + width], start=True, stop=True)
                last.then_inc(first_out, 1)

            def second_scores(n, j, step):
                (k0, q0, width), i = K_ITEM[j % 2], n // 2
                if j == 0:
                    step.wait(pe, max_loaded, 16 * (n + 1), 32)
                step.wait(pe, exp_done, ITEMS * n + j - 1, 2 * ITEMS)
                at = (n % 2) * SEQ
                for u in range(2):
                    h = 2 * (j // 2) + u
                    last = nc.tensor.matmul(second_bank[j % 2][:, u * 256:u * 256 + width],
                                            stack[i % 2][0:ROWS_K, h, 1, at + k0:at + k0 + P],
                                            stack[i % 2][0:ROWS_K, h, 0, at + q0:at + q0 + width], start=True, stop=True)
                last.then_inc(second_out, 1)

            def add_values(n, j, step):
                (_, q0, width), i = K_ITEM[j % 2], n // 2
                step.wait(pe, exp_done, ITEMS * n + j + 1, 2 * ITEMS)
                if j == 0:
                    if n % 2 == 0:
                        shared_wait_used(pe, [("v", i, 0), ("v", i, 1)], step)
                    step.wait(pe, att_taken, n - 1, 2)
                for u in range(2):
                    h = 2 * (j // 2) + u
                    group, place = h % GROUPS, h // GROUPS
                    row, col = 32 * (group % 4), SEQ * (group // 4) + q0
                    values = v_sb[i % 2][:, 2 * (n % 2) + j % 2, group, :, :].rearrange("p s e -> p (s e)")
                    last = nc.tensor.matmul(att_bank[n % 2][row:row + 2 * (DH + 1), col:col + width],
                                            values[:, place * (DH + 1):(place + 2) * (DH + 1)], probs[:, j % 4, u, 0:width],
                                            start=(h < 4 and j % 2 == 0), stop=(j % 2 == 1), skip_group_check=True)
                last.then_inc(att_added, 1)

            def turn(n, step):
                b = shared_open(pe, ("turn", n, 0), step)
                step.wait(pe, att_taken, n + 1, 2)
                for qt in range(2):
                    for s in range(2):
                        last = nc.tensor.transpose(shared_bank[b][:, (2 * qt + s) * P:(2 * qt + s + 1) * P],
                                                   att[:, s, qt * P:(qt + 1) * P], ident)
                last.then_inc(shared_out[b], 1)

            def back(n, step):
                b = shared_open(pe, ("back", n, 0), step, after=[("turn", n, 0)])
                for qt in range(2):
                    last = nc.tensor.transpose(shared_bank[b][:, qt * P:(qt + 1) * P], att_n[:, qt, :], ident)
                last.then_inc(shared_out[b], 1)

            def sum_rest(n, step):
                i = n // 2
                b = shared_open(pe, ("sum", n, 0), step, after=[("back", n, 0), ("up", i, 0), ("up", i, 1)])
                for qt in range(2):
                    into = shared_bank[b][:, qt * D:(qt + 1) * D]
                    nc.tensor.matmul(into, att_nT[:, qt, :], wo_sb[:, :], start=True, stop=False)
                    at = (n % 2) * SEQ + qt * P
                    for f in range(2):
                        last = nc.tensor.matmul(into, hT[:, i % 2, f, at:at + P], wd_sb[:, f * D:(f + 1) * D],
                                                start=False, stop=(f == 1))
                last.then_inc(shared_out[b], 1)

            def turn_max(n, step):
                step.wait(pe, max_split, n + 1, 2)
                b = shared_open(pe, ("max", n, 0), step)
                pass_wait(pe)
                view = shared_bank[b][:, :].bitcast(BF16)
                for qt in range(2):
                    last = nc.tensor.transpose(view[0:3 * HEADS, qt * P:(qt + 1) * P],
                                               max_parts[:, qt, :, :].rearrange("p a h -> p (a h)"), ident_bf[:, :])
                last.then_inc(shared_out[b], 1)

            def shared_use(what, of, part, step):
                if what in ("q", "k"):
                    project(what, of, step)
                elif what == "v":
                    project_v(of, part, step)
                elif what in ("gate", "up"):
                    gate_up(what, of, part, step)
                else:
                    {"turn": turn, "back": back, "sum": sum_rest, "max": turn_max}[what](of, step)

            plain = Step()
            for i in (0, 1):
                project("q", i, plain)
                project("k", i, plain)
            pe.wait_ge(counted, 1)
            nc.tensor.matmul(second_bank[0][:, 0:E], before, row_count[:, 0:E], start=True, stop=True)
            nc.tensor.matmul(second_bank[0][:, E:2 * E], ones[:, :], row_count[:, 0:E], start=True, stop=True).then_inc(ranked, 1)
            pe.wait_ge(routed, 1)
            for j in range(ITEMS):
                first_scores(0, j, plain)
            turn_max(0, plain)
            for use in [("v", 0, 0), ("v", 0, 1), ("gate", 0, 0), ("up", 0, 0), ("gate", 0, 1), ("up", 0, 1)]:
                shared_use(*use, plain)
            for j in range(LEAD):
                first_scores(1, j, plain)

            def batch(n, i, step):
                for j in range(ITEMS):
                    ahead_n, ahead_j = n + 1 + (j + LEAD) // ITEMS, (j + LEAD) % ITEMS
                    if ahead_n < BATCHES:
                        first_scores(ahead_n, ahead_j, step)
                    second_scores(n, j, step)
                    if j >= 2:
                        add_values(n, j - 2, step)
                    elif n >= 1:
                        add_values(n - 1, ITEMS - 2 + j, step)
                    for use in shared_uses_after(n, j):
                        shared_use(*use, step)

            def pair(i, step):
                batch(2 * i, i, step)
                batch(2 * i + 1, i, step)

            over_pairs(pe, pair)
            add_values(BATCHES - 1, ITEMS - 2, plain)
            add_values(BATCHES - 1, ITEMS - 1, plain)
            for what in ("turn", "back", "sum"):
                shared_use(what, BATCHES - 1, 0, plain)

            pe.wait_ge(experts_loaded, 32)

            experts = {}

            def expert_tile(s, ahead):
                if s % 8 == 0:
                    at = expert_of[0:1, s:s + 10] if ahead is None else expert_of[0:1, bass.ds(ahead + s, 10)]
                    _, got = nc.values_load_multi_w_load_instructions(at, engines=[pe.engine], min_val=0, max_val=EXPERTS - 1)
                    experts.update({s - 2 + k: e for k, e in enumerate(got)})

                def turn_row(s):
                    if ahead is None:
                        pe.wait_ge(row_loaded[s % 8], 16 * (s // 8 + 1))
                    else:
                        pe.wait_ge(row_loaded[s % 8], ahead * 2 + 16 * (s // 8 + 1))
                    wait_count(pe, rowT_done, s - 1, ahead)
                    nc.tensor.transpose(second_bank[s % 2][:, 0:P], ring[:, s % 8, 0:D], ident).then_inc(row_turned, 1)

                def turn_h(s):
                    wait_count(pe, h_done, s + 1, ahead)
                    wait_count(pe, e_hT_done, s - 1, ahead)
                    for f in range(2):
                        last = nc.tensor.transpose(att_bank[s % 2][:, f * P:(f + 1) * P], e_h[:, s % 2, f * P:(f + 1) * P], ident)
                    last.then_inc(h_turned, 1)

                def down(s):
                    wait_count(pe, e_hT_done, s + 1, ahead)
                    wait_count(pe, y_done, s - 1, ahead)
                    for f in range(2):
                        last = nc.tensor.matmul(shared_bank[s % 2][:, 0:D], e_hT[:, s % 2, f * P:(f + 1) * P],
                                                dn_sb[:, bass.ds(experts[s] * (2 * D) + f * D, D)], start=(f == 0), stop=(f == 1))
                    last.then_inc(y_out, 1)

                if s == 0 and ahead is None:
                    turn_row(0)
                if s + 1 < SORTED:
                    turn_row(s + 1)
                wait_count(pe, rowT_done, s + 1, ahead)
                wait_count(pe, h_done, s - 1, ahead)
                nc.tensor.matmul(first_bank[s % 2][:, :], rowT[:, s % 2, :], gu_sb[:, bass.ds(experts[s] * (2 * F), 2 * F)],
                                 start=True, stop=True).then_inc(gu_out, 1)
                if s >= 1:
                    turn_h(s - 1)
                if s >= 2:
                    down(s - 2)
                if s == SORTED - 1:
                    turn_h(s)
                    down(s - 1)
                    down(s)

            over_sorted(pe, expert_tile)

        @block.vector
        def _(dve):
            own = Count(dve, dve_own)
            nc.vector.memset(ones[:, :], 1.0)
            for b in range(2):
                nc.vector.memset(att_bank[b][:, :], 0.0)
                nc.vector.memset(v_sb[b][:, :, :, :, :], 0.0)
            own.link(nc.vector.memset(expert_of[:, :], 0))
            for b in range(2):
                nc.vector.memset(v_sb[b][:, :, :, :, DH:DH + 1], 1.0)

            def take_stats(c, half, b, ring4, runtime):
                dve.wait_ge(x_loaded[b], half)
                for k in range(PT):
                    src = x_res[:, bass.ds(c * PT + k, 1), :] if runtime else x_res[:, c * PT + k:c * PT + k + 1, :]
                    last = nc.vector.bn_stats(stats[:, b, k, :], src.rearrange("p a d -> p (a d)"))
                last.then_inc(stats_done, 1)
                dve.wait_ge(stats_done, c + 1)
                pass_wait(dve)
                for k in range(PT):
                    last = nc.vector.bn_aggr(moments[:, ring4, k, :], stats[:, b, k, :])
                last.then_inc(moments_done, 1)

            def norm(c, b, ring4, runtime):
                dve.wait_ge(rstd_done, c + 1)
                if runtime or c >= 2:
                    dve.wait_ge(xn_turned, c - 1)
                for k in range(PT):
                    t = c * PT + k
                    src = x_res[:, bass.ds(t, 1), :].rearrange("p a d -> p (a d)") if runtime else x_res[:, t, :]
                    r = rstd[:, bass.ds(t, 1)] if runtime else rstd[:, t:t + 1]
                    last = nc.vector.tensor_scalar(xn[b][:, k, :], src, moments[:, ring4, k, 0:1], r, ALU.subtract, ALU.mult)
                last.then_inc(xn_done, 1)

            for c in range(4):
                take_stats(c, 16 * (c // 2 + 1), c % 2, c % 4, False)
                if c >= 1:
                    norm(c - 1, (c - 1) % 2, (c - 1) % 4, False)
            with dve.Fori(0, PAIRS // 4 - 1) as turn:
                for c in range(4, 8):
                    take_stats(turn * 4 + c, turn * 32 + 16 * (c // 2 + 1), c % 2, c % 4, True)
                    norm(turn * 4 + (c - 1), (c - 1) % 2, (c - 1) % 4, True)
            norm(PAIRS - 1, 1, 3, False)

            dve.wait_ge(weights_loaded, 16 * 12)
            nc.vector.tensor_scalar(bqs[:, :], bq_sb[:, :], DH**-0.5, None, ALU.mult)
            nc.vector.tensor_copy(ident_bf[:, :], ident).then_inc(prepared, 1)

            def take_v(i, half, step):
                b = shared_wait_out(dve, [("v", i, half)], step)
                by_place = "p (s g d) -> p g s d"
                for k in range(2):
                    last = nc.vector.tensor_tensor(v_sb[i % 2][:, 2 * half + k, :, :, 0:DH],
                                                   shared_bank[b][:, k * D:(k + 1) * D].rearrange(by_place, s=2, d=DH),
                                                   bv_sb[:, :].rearrange(by_place, s=2, d=DH), ALU.add)
                last.then_inc(shared_used[b], 1)

            def over_experts(ap):
                return ap.unsqueeze(2).to_broadcast([P, T, E])

            def over_tiles(ap):
                return ap.unsqueeze(1).to_broadcast([P, T, E])

            plain = Step()
            dve.wait_ge(logits_done, PAIRS)
            top_ins = nc.vector.tensor_reduce(top[:, 0:T], logits, AX.X, ALU.max)
            top_ins.then_inc(top_done, 1)
            dve.wait_ge(top_done, 1)
            own.link(nc.vector.tensor_tensor(work, logits, over_experts(top[:, 0:T]), ALU.is_equal))
            own.link(nc.vector.tensor_tensor(work, work, over_tiles(rev), ALU.mult))
            own.link(nc.vector.tensor_reduce(first[:, 0:T], work, AX.X, ALU.max))
            own.link(nc.vector.tensor_tensor(hot, over_tiles(rev), over_experts(first[:, 0:T]), ALU.is_equal))
            nc.vector.tensor_reduce(row_count[:, 0:E], hot.rearrange("p t e -> p e t"), AX.X, ALU.add).then_inc(counted, 1)
            src = hot
            for k, s in enumerate((1, 2, 4, 8, 16, 32)):
                dst = (tally_a, tally_b)[k % 2]
                nc.vector.tensor_copy(dst[:, 0:s, :], src[:, 0:s, :])
                own.link(nc.vector.tensor_tensor(dst[:, s:T, :], src[:, s:T, :], src[:, 0:T - s, :], ALU.add))
                src = dst
            tally = src
            dve.wait_ge(ranked, 1)
            own.link(nc.vector.tensor_copy(slot_f[:, 0:E], second_bank[0][:, E:2 * E]))
            exceeds = work.rearrange("p t e -> p (t e)").rearrange("p (e t) -> p e t", e=E)
            own.link(nc.vector.tensor_tensor(exceeds, slot_f[:, 0:E].unsqueeze(2).to_broadcast([P, E, T]),
                                             steps128.unsqueeze(1).to_broadcast([P, E, T]), ALU.is_gt))
            own.link(nc.vector.tensor_reduce(n_tiles[:, 0:E], exceeds, AX.X, ALU.add))
            src = n_tiles
            for k, s in enumerate((1, 2, 4, 8)):
                dst = (ends_a, ends_b)[k % 2]
                nc.vector.tensor_copy(dst[:, 0:s], src[:, 0:s])
                own.link(nc.vector.tensor_tensor(dst[:, s:E], src[:, s:E], src[:, 0:E - s], ALU.add))
                src = dst
            ends = src
            own.link(nc.vector.tensor_tensor(base[:, 0:E], ends[:, 0:E], n_tiles[:, 0:E], ALU.subtract))
            own.link(nc.vector.tensor_scalar(base[:, 0:E], base[:, 0:E], float(P), -1.0, ALU.mult, ALU.add))
            own.link(nc.vector.tensor_tensor(base[:, 0:E], second_bank[0][:, 0:E], base[:, 0:E], ALU.add))
            own.link(nc.vector.tensor_tensor(work, tally, over_tiles(base[:, 0:E]), ALU.add))
            own.link(nc.vector.tensor_tensor(work, work, hot, ALU.mult))
            own.link(nc.vector.tensor_reduce(slot_f[:, 0:T], work, AX.X, ALU.add))
            nc.vector.tensor_copy(slot[:, :], slot_f[:, 0:T])
            own.link(nc.vector.tensor_tensor(compare, tile_no.unsqueeze(2).to_broadcast([P, SORTED, E]),
                                             ends[:, 0:E].unsqueeze(1).to_broadcast([P, SORTED, E]), ALU.is_ge))
            own.link(nc.vector.tensor_reduce(ends_a[:, 0:SORTED] if ends is ends_b else ends_b[:, 0:SORTED], compare, AX.X, ALU.add))
            which = ends_a if ends is ends_b else ends_b
            nc.vector.tensor_scalar(expert_of[:, 2:2 + SORTED], which[:, 0:SORTED], float(E - 1), None, ALU.min)
            dve.wait_ge(exp_top_done, 1)
            own.link(nc.vector.tensor_scalar(score[:, 0:T], score[:, 0:T], 1.0, None, ALU.add))
            own.link(nc.vector.reciprocal(score[:, 0:T], score[:, 0:T]))
            own.link(nc.vector.tensor_tensor(send_scale[:, :], score[:, 0:T], rstd[:, :], ALU.mult))
            nc.vector.scalar_tensor_tensor(send_shift[:, :], mean[:, :], -1.0, send_scale[:, :], ALU.mult, ALU.mult).then_inc(routed, 1)

            def take_first(n, j, step):
                width = Q_ITEM[j % 2][2]
                step.wait(dve, first_out, ITEMS * n + j + 1, 2 * ITEMS)
                if j == 0:
                    step.wait(dve, max_split, n - 1, 2)
                nc.vector.tensor_reduce(neg_max[:, n % 2, j % 2, 2 * (j // 2):2 * (j // 2) + 2],
                                        first_bank[j % 2][:, :].rearrange("p (u w) -> p u w", u=2)[:, :, 0:width],
                                        AX.X, ALU.max, negate=True).then_inc(max_taken, 1)

            def split_max(n, step):
                step.wait(dve, max_taken, ITEMS * (n + 1), 2 * ITEMS)
                wait_last(dve, shared_out, [("max", n - 1, 0)], step)
                full = neg_max[:, n % 2, :, :]
                own.link(nc.vector.tensor_copy(max_parts[:, :, 0, :], full))
                own.link(nc.vector.tensor_tensor(full, full, max_parts[:, :, 0, :], ALU.subtract))
                own.link(nc.vector.tensor_copy(max_parts[:, :, 1, :], full))
                nc.vector.tensor_tensor(max_parts[:, :, 2, :], full, max_parts[:, :, 1, :],
                                        ALU.subtract).then_inc(max_split, 1)

            def normalise(n, step):
                b = shared_wait_out(dve, [("turn", n, 0), ("back", n - 1, 0)], step)
                heads = shared_bank[b][:, :].rearrange("p (g r) -> p g r", r=32)[:, :, 0:2 * (DH + 1)]
                heads = heads.rearrange("p g (s e) -> p g s e", s=2)
                nc.vector.reciprocal(recip[:, :, :], heads[:, :, :, DH]).then_inc(recip_done, 1)
                step.wait(dve, recip_done, n + 1, 2)
                nc.vector.tensor_tensor(att_n[:, :, :].rearrange("p q (g s d) -> p (q g) s d", s=2, d=DH), heads[:, :, :, 0:DH],
                                        recip[:, :, :].unsqueeze(3).to_broadcast([P, 2 * GROUPS, 2, DH]), ALU.mult).then_inc(shared_used[b], 1)

            def add_rest(n, step):
                b = shared_wait_out(dve, [("sum", n, 0)], step)
                if n % 2 == 0:
                    step.wait(dve, send_made, n // 2 + 1, 1)
                at = x_res[:, 2 * n:2 * n + 2, :] if step.ahead is None else x_res[:, bass.ds(step.ahead * PT + 2 * n, 2), :]
                nc.vector.tensor_tensor(at, shared_bank[b][:, 0:2 * D].rearrange("p (q d) -> p q d", q=2), at, ALU.add).then_inc(shared_used[b], 1)

            def take_gate(i, f, step):
                b = shared_wait_out(dve, [("gate", i, f)], step)
                step.wait(dve, tanh_done, 2 * i + f + 1, 2)
                shared_wait_used(dve, [("up", i + f - 1, 1 - f)], step)
                nc.vector.scalar_tensor_tensor(gated[:, :], th[:, :], 1.0, shared_bank[b][:, :], ALU.add, ALU.mult).then_inc(shared_used[b], 1)

            def take_up(i, f, step):
                shared_wait_used(dve, [("gate", i, f)], step)
                b = shared_wait_out(dve, [("up", i, f), ("sum", 2 * i - 3, 0)], step)
                nc.vector.scalar_tensor_tensor(hT[:, i % 2, f, :], gated[:, :], 0.5, shared_bank[b][:, :], ALU.mult, ALU.mult).then_inc(shared_used[b], 1)

            def batch(n, i, step):
                for j in range(ITEMS):
                    ahead_n, ahead_j = n + 1 + (j + LEAD) // ITEMS, (j + LEAD) % ITEMS
                    if ahead_n < BATCHES:
                        take_first(ahead_n, ahead_j, step)
                        if ahead_j == ITEMS - 1:
                            split_max(ahead_n, step)
                    if n >= 1 and j == 4:
                        normalise(n - 1, step)
                    if n >= 1 and j == 10:
                        add_rest(n - 1, step)
                    if n % 2 == 1 and i + 1 < PAIRS:
                        if j in (1, 11):
                            take_gate(i + 1, (1, 11).index(j), step)
                        if j in (2, 14):
                            take_up(i + 1, (2, 14).index(j), step)
                    if n % 2 == 0 and i + 1 < PAIRS and j in (2, 6):
                        take_v(i + 1, (2, 6).index(j), step)

            for j in range(ITEMS):
                take_first(0, j, plain)
            split_max(0, plain)
            take_v(0, 0, plain)
            take_v(0, 1, plain)
            for f in range(2):
                take_gate(0, f, plain)
                take_up(0, f, plain)
            for j in range(LEAD):
                take_first(1, j, plain)

            def pair(i, step):
                batch(2 * i, i, step)
                batch(2 * i + 1, i, step)

            over_pairs(dve, pair, own, 4 * 3)
            normalise(BATCHES - 1, plain)
            add_rest(BATCHES - 1, plain)

            def expert_tile(s, ahead):
                wait_count(dve, e_tanh_done, s + 1, ahead)
                wait_count(dve, h_done, s - 1, ahead)
                nc.vector.scalar_tensor_tensor(e_gated[:, s % 2, :], e_th[:, s % 2, :], 1.0, first_bank[s % 2][:, 0:F], ALU.add, ALU.mult).then_inc(e_gated_done, 1)
                wait_count(dve, e_gated_done, s + 1, ahead)
                wait_count(dve, h_turned, s - 1, ahead)
                nc.vector.tensor_tensor(e_h[:, s % 2, :], first_bank[s % 2][:, F:2 * F], e_gated[:, s % 2, :], ALU.mult).then_inc(h_done, 1)

                def take_y(s):
                    wait_count(dve, y_out, s + 1, ahead)
                    if ahead is not None or s >= 4:
                        dve.wait_ge(y_sent[s % 4], plus(s // 4 * 16, ahead, 4))
                    nc.vector.tensor_copy(e_y[:, s % 4, :], shared_bank[s % 2][:, 0:D]).then_inc(y_done, 1)

                if s >= 2:
                    take_y(s - 2)
                if s == SORTED - 1:
                    take_y(s - 1)
                    take_y(s)

            over_sorted(dve, expert_tile)

            dve.wait_ge(bo_added, PAIRS)

            def add_back(c, ahead):
                if ahead is None:
                    dve.wait_ge(back_loaded[c % 4], 16 * (c // 4 + 1))
                    at = x_res[:, c * PT:c * PT + PT, :]
                else:
                    dve.wait_ge(back_loaded[c % 4], ahead * 4 + 16 * (c // 4 + 1))
                    at = x_res[:, bass.ds(ahead * PT + c * PT, PT), :]
                nc.vector.tensor_tensor(at, at, fetched[:, c % 4, :, :], ALU.add).then_inc(all_added, 1)

            with dve.Fori(0, PAIRS // 4) as turn:
                for c in range(4):
                    add_back(c, turn * 4)


def constants():
    p = np.arange(P)
    rev = np.broadcast_to(EXPERTS - np.arange(EXPERTS), (P, EXPERTS))
    steps128 = np.broadcast_to(P * np.arange(TILES), (P, TILES))
    tile_no = np.broadcast_to(np.arange(SORTED), (P, SORTED))
    cst = np.concatenate([np.eye(P), p[:, None] < p[None, :], rev, steps128, tile_no], 1).astype(np.float32)
    mask_q, mask_k = np.zeros((P, PAIR), np.float32), np.zeros((P, PAIR), np.float32)
    pos = np.arange(PAIR) % SEQ
    blk, off = pos // WINDOW, pos % WINDOW
    for r, row in enumerate(FINE_ROWS):
        parity, key = r // WINDOW, r % WINDOW
        allowed = np.where(blk % 2 == parity, key <= off, key > off)
        mask_q[row] = np.where(allowed, 0.0, FAR)
        mask_k[row] = (blk % 2 == parity) & (off == key)
    for b, row in enumerate(BLOCK_ROWS):
        mask_q[row] = np.where((b == blk) | (b == blk - 1), 0.0, FAR)
        mask_k[row] = blk == b
    mask_k[MAX_ROW:MAX_ROW + 3] = 1.0
    tok = (np.arange(TILES)[None, :] * P + p[:, None]).astype(np.int32)
    mask_q, mask_k = ((m.view(np.uint32) >> 16).astype(np.uint16) for m in (mask_q, mask_k))
    return cst, mask_q, mask_k, tok


def kernel(**inputs):
    import concourse.bacc as _bacc
    from concourse.bass_utils import run_bass_kernel_spmd as _run

    g = {k.removeprefix("L0_"): np.asarray(v) for k, v in inputs.items()}

    def by_dim_then_head(w):
        return w.reshape(HEADS, DH, -1).swapaxes(0, 1).reshape(D, -1)

    cst, mask_q, mask_k, tok = constants()
    arrays = {
        "x": g["attn_x"].reshape(TOKENS, D),
        "wq": by_dim_then_head(g["attn_Wq"]).T, "bq": by_dim_then_head(g["attn_bq"]),
        "wk": by_dim_then_head(g["attn_Wk"]).T, "bk": by_dim_then_head(g["attn_bk"]),
        "wv": g["attn_Wv"].T, "bv": g["attn_bv"].reshape(1, D),
        "wo": g["attn_Wo"].T.reshape(2, GROUPS, DH, D).swapaxes(0, 1).reshape(D, D), "bo": g["attn_bo"].reshape(1, D),
        "wr": g["ffn_w_router"].T, "wgu": g["ffn_gate_up_proj"], "wdn": g["ffn_down_proj"],
        "wg": g["ffn_w_gate"].T, "wu": g["ffn_w_up"].T, "wd": g["ffn_w_down"].T,
        "cst": cst, "mask_q": mask_q, "mask_k": mask_k, "tok": tok,
    }
    nc = _bacc.Bacc("TRN2", target_bir_lowering=False, num_devices=1)
    args, given = [], {}
    for name, a in arrays.items():
        given[f"in_{name}"] = a = np.ascontiguousarray(a)
        args.append(nc.dram_tensor(f"in_{name}", list(a.shape), mybir.dt.from_np(a.dtype), kind="ExternalInput").ap())
    out = nc.dram_tensor("out_0", [TOKENS, D], F32, kind="ExternalOutput").ap()
    build(nc, *args, out)
    r = _run(nc, [given], core_ids=[0])
    return r.results[0]["out_0"].reshape(BATCHES, SEQ, D)
```

```python
from contextlib import ExitStack

import concourse.bass as bass
import numpy as np
from concourse import mybir

F32, BF16 = mybir.dt.float32, mybir.dt.bfloat16
I32, U32, U16 = mybir.dt.int32, mybir.dt.uint32, mybir.dt.uint16
ALU = mybir.AluOpType
ACT = mybir.ActivationFunctionType
AX = mybir.AxisListType

P = 128
BATCHES, SEQ, D = 32, 256, 128
HEADS, DH, WINDOW = 16, 8, 32
EXPERTS, F = 16, 256
GROUPS = HEADS // 2
TOKENS = BATCHES * SEQ
TILES = TOKENS // P
PAIR = 2 * SEQ
PAIRS = TOKENS // PAIR
PT = PAIR // P
SORTED = TILES + EXPERTS
EPS = 1e-5
FAR = -float(2.0**100)
ROW = D + 4

PART_ROWS = [0, 8, 16, 64, 72, 80]
Q_PARTS = [0, 0, 1, 1, 0, 2]
K_PARTS = [0, 1, 0, 1, 2, 0]
FINE_ROWS = list(range(24, 64)) + list(range(88, 112))
BLOCK_ROWS = list(range(112, 120))
MAX_ROW = 120
ROWS_Q, ROWS_K = 120, 123
NORM_BEFORE = 12
MASK_ROWS = [slice(24, 64), slice(88, 123)]

Q_ITEM = [(0, 0, 128), (128, 96, 160)]
K_ITEM = [(0, 0, 160), (128, 128, 128)]
ITEMS = 16
LEAD = 7
POST = {3: "turn", 6: "back", 8: "sum", 10: "max"}
EVEN = {1: ("v", 0), 5: ("v", 1), 12: ("q", 0), 14: ("k", 0)}
ODD = {0: ("gate", 0), 1: ("up", 0), 11: ("gate", 1), 13: ("up", 1)}
ROUTE_AT = [(0, 1), (0, 3), (0, 5), (0, 7), (0, 11), (0, 13), (1, 4), (1, 6), (1, 7), (1, 8), (1, 13),
            (2, 1), (2, 3), (2, 7), (2, 11), (2, 13), (3, 4), (3, 7), (3, 12), (3, 15)]
RANK_AT = (0, 15)


FIRST_USES = [("v", 0, 0), ("v", 0, 1), ("gate", 0, 0), ("up", 0, 0), ("gate", 0, 1), ("up", 0, 1)]


def shared_uses_after(n, j):
    uses, i = [], n // 2
    if (n, j) == RANK_AT:
        uses.append(("rank", 0, 0))
    if j in POST:
        of = n + 1 if POST[j] == "max" else n - 1
        if 0 <= of < BATCHES:
            uses.append((POST[j], of, 0))
    for when in (EVEN, ODD)[n % 2].items():
        if when[0] == j:
            what, part = when[1]
            of = i + 2 if what in "qk" else i + 1
            if of < PAIRS:
                uses.append((what, of, part))
    return uses


def shared_bank_order():
    order = [("q", 0, 0), ("k", 0, 0), ("q", 1, 0), ("k", 1, 0), *FIRST_USES, ("max", 0, 0)]
    for n in range(BATCHES):
        for j in range(ITEMS):
            order += shared_uses_after(n, j)
    order += [(what, BATCHES - 1, 0) for what in ("turn", "back", "sum")]
    return {use: at for at, use in enumerate(order)}


SHARED = shared_bank_order()
SHARED_PER_PAIR = 16


class Step:

    def __init__(self, ahead=None):
        self.ahead = ahead

    def value(self, at_ref, per_pair):
        return at_ref if self.ahead is None else at_ref + self.ahead * per_pair

    def wait(self, eng, sem, at_ref, per_pair):
        if self.ahead is not None or at_ref > 0:
            eng.wait_ge(sem, self.value(at_ref, per_pair))


class Count:

    def __init__(self, eng, sem):
        self.eng, self.sem, self.n, self.extra = eng, sem, 0, None

    def link(self, ins):
        ins.then_inc(self.sem, 1)
        self.n += 1
        self.eng.wait_ge(self.sem, self.n if self.extra is None else self.extra + self.n)

    def mark(self, ins):
        ins.then_inc(self.sem, 1)
        self.n += 1

    def settle(self):
        self.eng.wait_ge(self.sem, self.n)

    def enter(self, turn, per_turn):
        self.extra, self.start, self.per_turn = turn * per_turn, self.n, per_turn

    def leave(self, turns):
        assert self.n - self.start == self.per_turn, (self.n - self.start, self.per_turn)
        self.n, self.extra = self.start + turns * self.per_turn, None


def build(nc, x, wq, bq, wk, bk, wv, bv, wo, bo, wr, wgu, wdn, wg, wu, wd, cst, mask_q, mask_k, tok, out):
    ctx = ExitStack()
    with ctx:
        def sb(name, shape, dt=F32):
            return ctx.enter_context(nc.sbuf_tensor(name, shape, dt))

        def sem(name):
            return ctx.enter_context(nc.semaphore(name))

        xnT_dram = nc.dram_tensor("xnT_keep", [PAIRS, P, PAIR], F32).ap()
        sorted_dram = nc.dram_tensor("sorted_keep", [SORTED * P, ROW], F32).ap()

        x_res = sb("x_res", [P, TILES, D])
        stack = [sb(f"stack{b}", [P, HEADS, 2, PAIR], BF16) for b in range(2)]
        gu_sb = sb("gu_sb", [P, EXPERTS * 2 * F])
        dn_sb = sb("dn_sb", [P, EXPERTS * 2 * D])
        v_sb = [sb(f"v_sb{b}", [P, PT, GROUPS, 2, 2 * (DH + 1)]) for b in range(2)]
        xnT = [sb(f"xnT{b}", [P, PAIR]) for b in range(2)]
        q32 = sb("q32", [P, PAIR])
        k32 = sb("k32", [P, PAIR])
        parts = sb("parts", [P, 6, PAIR], BF16)
        probs = sb("probs", [P, 4, 2, 160])
        att = sb("att", [P, 2, SEQ])
        att_n = sb("att_n", [P, 2, D])
        att_nT = sb("att_nT", [P, 2, P])
        recip = sb("recip", [P, 2 * GROUPS, 2])
        neg_max = sb("neg_max", [P, 2, 2, HEADS])
        max_parts = sb("max_parts", [P, 2, 3, HEADS], BF16)
        maxT = sb("maxT", [3 * HEADS, SEQ], BF16)
        th = sb("th", [P, PAIR])
        gated = sb("gated", [P, PAIR])
        hT = sb("hT", [P, 2, 2, PAIR])
        wq_sb, wk_sb, wv_sb, wo_sb = (sb(n, [P, D]) for n in ("wq_sb", "wk_sb", "wv_sb", "wo_sb"))
        wr_sb = sb("wr_sb", [P, EXPERTS])
        wg_sb, wu_sb, wd_sb = (sb(n, [P, F]) for n in ("wg_sb", "wu_sb", "wd_sb"))
        bq_sb, bk_sb, bqs = (sb(n, [P, 1]) for n in ("bq_sb", "bk_sb", "bqs"))
        bv_sb, bo_sb = sb("bv_sb", [P, D]), sb("bo_sb", [P, D])
        cst_sb = sb("cst_sb", [P, cst.shape[1]])
        ident, before = cst_sb[:, 0:P], cst_sb[:, P:2 * P]
        rev = cst_sb[:, 2 * P:2 * P + EXPERTS]
        steps128 = cst_sb[:, 2 * P + EXPERTS:2 * P + EXPERTS + TILES]
        tile_no = cst_sb[:, 2 * P + EXPERTS + TILES:2 * P + EXPERTS + TILES + SORTED]
        ident_bf = sb("ident_bf", [P, P], BF16)
        mask_q_sb, mask_k_sb = sb("mask_q_sb", [P, PAIR], BF16), sb("mask_k_sb", [P, PAIR], BF16)
        tok_sb = sb("tok_sb", [P, TILES], I32)
        ones = sb("ones", [P, P])
        stats = sb("stats", [P, 2, PT, 6])
        moments = sb("moments", [P, 4, PT, 2])
        var_eps = sb("var_eps", [P, PT])
        neg_half = sb("neg_half", [P, PT])
        mean, rstd = sb("mean", [P, TILES]), sb("rstd", [P, TILES])
        slot = sb("slot", [P, TILES], I32)
        send_scale, send_shift = sb("send_scale", [P, TILES]), sb("send_shift", [P, TILES])
        send = sb("send", [P, 2, PT, ROW])
        blank = sb("blank", [P, ROW])
        ranks = sb("ranks", [P, 2 * EXPERTS])
        expert_of = sb("expert_of", [P, SORTED + 4], I32)

        def scratch(at, *shape):
            n = int(np.prod(shape))
            ap = gu_sb[:, at:at + n]
            return ap if len(shape) == 1 else ap.rearrange("p (a b) -> p a b", b=shape[1])

        def scratch_bf(at, *shape):
            ap = gu_sb[:, at:at + int(np.prod(shape)) // 2].bitcast(BF16)
            return ap if len(shape) == 1 else ap.rearrange("p (a b) -> p a b", b=shape[1])

        E, T = EXPERTS, TILES
        xn = [scratch(b * PAIR, PT, D) for b in range(2)]
        logits = scratch(1024, T, E)
        work = scratch(2048, T, E)
        hot, tally_a, tally_b, marks = (scratch_bf(3072 + 512 * k, T, E) for k in range(4))
        compare = scratch_bf(5120, SORTED, E)
        rev_bf, tile_bf, first, ends_bf = (scratch_bf(5760 + 80 * k, 160) for k in range(4))
        small = [scratch(7424 + 80 * k, 80) for k in range(8)]
        top, score, row_count, n_tiles, ends_a, ends, base, slot_f = small
        late, late2 = (stack[b][:, :, :, :].rearrange("p h c n -> p (h c n)").bitcast(F32) for b in range(2))
        ring = late[:, 0:8 * ROW].rearrange("p (r c) -> p r c", c=ROW)
        rowT = late[:, 1100:1100 + 2 * P].rearrange("p (r c) -> p r c", c=P)
        e_th = late[:, 1400:1400 + 2 * F].rearrange("p (r c) -> p r c", c=F)
        e_gated = late2[:, 2100:2100 + 2 * F].rearrange("p (r c) -> p r c", c=F)
        e_h = late[:, 2300:2300 + 2 * F].rearrange("p (r c) -> p r c", c=F)
        e_hT = late[:, 2900:2900 + 2 * F].rearrange("p (r c) -> p r c", c=F)
        e_y = late[:, 3500:3500 + 4 * D].rearrange("p (r c) -> p r c", c=D)
        chunkT = [dn_sb[:, b * PAIR:(b + 1) * PAIR] for b in range(2)]

        bank = [ctx.enter_context(nc.psum_tensor(f"bank{b}", [P, 512], F32)) for b in range(8)]
        first_bank, second_bank, att_bank, shared_bank = bank[0:2], bank[2:4], bank[4:6], bank[6:8]

        x_loaded = [sem(f"x_loaded{b}") for b in range(4)]
        const_loaded, weights_loaded = sem("const_loaded"), sem("weights_loaded")
        masks_loaded, stacks_masked = sem("masks_loaded"), sem("stacks_masked")
        blank_made, blanks_stored = sem("blank_made"), sem("blanks_stored")
        prepared, waits_passed = sem("prepared"), sem("waits_passed")
        stats_done, moments_done, rstd_done = sem("stats_done"), sem("moments_done"), sem("rstd_done")
        xn_done, xn_turned, xnT_done = sem("xn_done"), sem("xn_turned"), sem("xnT_done")
        xnT_stored = [sem(f"xnT_stored{b}") for b in range(2)]
        logits_out, logits_done = sem("logits_out"), sem("logits_done")
        top_done, exp_top_done, counted, routed = (
            sem(n) for n in ("top_done", "exp_top_done", "counted", "routed"))
        dve_own, pool_own = sem("dve_own"), sem("pool_own")
        send_made = sem("send_made")
        sent = [sem(f"sent{b}") for b in range(2)]
        experts_loaded = sem("experts_loaded")
        xnT_loaded = [sem(f"xnT_loaded{b}") for b in range(2)]
        parts_made = sem("parts_made")
        stack_loaded = [sem(f"stack_loaded{b}") for b in range(2)]
        first_out, max_taken = sem("first_out"), sem("max_taken")
        second_out, exp_done, att_added, att_taken = (
            sem(n) for n in ("second_out", "exp_done", "att_added", "att_taken"))
        shared_out = [sem(f"shared_out{b}") for b in range(2)]
        shared_used = [sem(f"shared_used{b}") for b in range(2)]
        max_split, max_loaded = sem("max_split"), sem("max_loaded")
        recip_done, tanh_done, bo_added = sem("recip_done"), sem("tanh_done"), sem("bo_added")
        row_loaded = [sem(f"row_loaded{r}") for r in range(8)]
        row_turned, rowT_done, gu_out, e_tanh_done, e_gated_done, h_done = (
            sem(n) for n in ("row_turned", "rowT_done", "gu_out", "e_tanh_done", "e_gated_done", "h_done"))
        h_turned, e_hT_done, y_out, y_done = (sem(n) for n in ("h_turned", "e_hT_done", "y_out", "y_done"))
        y_sent = [sem(f"y_sent{r}") for r in range(4)]
        out_stored, last_stored = sem("out_stored"), sem("last_stored")
        v_zeroed = sem("v_zeroed")

        block = ctx.enter_context(nc.Block())

        x_by_chunk = x.rearrange("(c k p) d -> c p k d", p=P, k=PT)
        out_by_chunk = out.rearrange("(c k p) d -> c p k d", p=P, k=PT)

        def wait_last(eng, sems, uses, step):
            last = {}
            for use in uses:
                if use in SHARED:
                    b = SHARED[use] % 2
                    last[b] = max(last.get(b, 0), SHARED[use] // 2 + 1)
            for b, at in last.items():
                step.wait(eng, sems[b], at, SHARED_PER_PAIR // 2)

        def shared_wait_out(eng, uses, step):
            wait_last(eng, shared_out, uses, step)
            return SHARED[uses[0]] % 2

        def shared_wait_used(eng, uses, step):
            wait_last(eng, shared_used, uses, step)

        def shared_open(pe, use, step, after=()):
            at = SHARED[use]
            assert all(SHARED[a] < at for a in after)
            before = [a for a, k in SHARED.items() if k == at - 2]
            wait_last(pe, shared_used, [*before, *after], step)
            return at % 2

        def over_pairs(eng, emit, count=None, per_turn=0):
            for i in (0, 1):
                emit(i, Step())
            with eng.Fori(0, 6) as turn:
                if count:
                    count.enter(turn, per_turn)
                for i in (2, 3):
                    emit(i, Step(turn * 2))
            if count:
                count.leave(6)
            for i in (14, 15):
                emit(i, Step())

        def over_sorted(eng, emit):
            for s in range(8):
                emit(s, None)
            with eng.Fori(0, SORTED // 8 - 2) as turn:
                for s in range(8, 16):
                    emit(s, turn * 8)
            for s in range(SORTED - 8, SORTED):
                emit(s, None)

        def pass_wait(eng):
            eng.sem_inc(waits_passed, 1)

        def plus(value, ahead, factor=1):
            return value if ahead is None else value + (ahead if factor == 1 else ahead * factor)

        def wait_count(eng, s, value, ahead):
            if ahead is not None or value > 0:
                eng.wait_ge(s, plus(value, ahead))

        @block.sync
        def _(sp):
            def load_x(c, b, runtime):
                to = x_res[:, bass.ds(c * PT, PT), :] if runtime else x_res[:, c * PT:c * PT + PT, :]
                src = x_by_chunk[bass.ds(c, 1), :, :, :].rearrange("a p k d -> (a p) k d") if runtime else x_by_chunk[c]
                sp.dma_start(to, src).then_inc(x_loaded[b], 16)

            for c in range(4):
                load_x(c, c, False)
            with sp.Fori(1, PAIRS // 4) as k:
                for b in range(4):
                    sp.wait_ge(x_loaded[b], k * 16)
                    pass_wait(sp)
                    load_x(k * 4 + b, b, True)

            def mask_stack(b):
                for c, mask in enumerate((mask_q_sb, mask_k_sb)):
                    for rows in MASK_ROWS:
                        sp.dma_start(stack[b][rows, :, c, :],
                                     mask[rows, :].unsqueeze(1).to_broadcast([rows.stop - rows.start, HEADS, PAIR])).then_inc(stacks_masked, 16)

            def load_xnT(i, step):
                if i >= 2:
                    shared_wait_out(sp, [("up", i - 2, 1)], step)
                    pass_wait(sp)
                src = xnT_dram[i] if step.ahead is None else xnT_dram[bass.ds(step.ahead + i, 1), :, :].rearrange("a p n -> (a p) n")
                sp.dma_start(xnT[i % 2][:, :], src).then_inc(xnT_loaded[i % 2], 16)

            def stack_parts(i, step):
                step.wait(sp, parts_made, 2 * i + 2, 2)
                pass_wait(sp)
                step.wait(sp, second_out, 2 * ITEMS * (i - 1), 2 * ITEMS)
                pass_wait(sp)
                for row, q_part, k_part in zip(PART_ROWS, Q_PARTS, K_PARTS):
                    both = parts[:, q_part:3 + k_part + 1:3 + k_part - q_part, :]
                    sp.dma_start(stack[i % 2][row:row + DH, :, :, :].rearrange("p h c n -> p (h c n)"), both).then_inc(stack_loaded[i % 2], 16)

            def stack_max(n, step):
                shared_wait_used(sp, [("max", n, 0)], step)
                half = (n % 2) * SEQ
                sp.dma_start(stack[(n // 2) % 2][MAX_ROW:MAX_ROW + 3, :, 0, half:half + SEQ], maxT[:, :]).then_inc(max_loaded, 16)

            def store_rest(i, step):
                step.wait(sp, bo_added, i + 1, 1)
                if step.ahead is None:
                    sp.dma_start(out_by_chunk[i], x_res[:, i * PT:i * PT + PT, :]).then_inc(out_stored, 16)
                else:
                    pass_wait(sp)
                    sp.dma_start(out_by_chunk[bass.ds(step.ahead + i, 1), :, :, :].rearrange("a p k d -> (a p) k d"),
                                 x_res[:, bass.ds(step.ahead * PT + i * PT, PT), :]).then_inc(out_stored, 16)

            plain = Step()
            for i in (0, 1):
                sp.wait_ge(xnT_stored[i], 16)
                load_xnT(i, plain)
            sp.wait_ge(masks_loaded, 32)
            mask_stack(0)
            sp.wait_ge(stacks_masked, 32 * len(MASK_ROWS))
            stack_parts(0, plain)
            mask_stack(1)
            for b in range(2):
                sp.wait_ge(xnT_stored[b], 16 * (PAIRS // 2))
            sp.wait_ge(stacks_masked, 2 * 32 * len(MASK_ROWS))
            stack_parts(1, plain)
            stack_max(0, plain)

            def pair(i, step):
                if 1 <= i < PAIRS - 1:
                    stack_parts(i + 1, step)
                if i + 2 < PAIRS:
                    load_xnT(i + 2, step)
                stack_max(2 * i + 1, step)
                if i + 1 < PAIRS:
                    stack_max(2 * i + 2, step)
                if i >= 1:
                    store_rest(i - 1, step)

            over_pairs(sp, pair)

            sp.wait_ge(second_out, ITEMS * (BATCHES - 2))
            for b in range(2):
                sp.wait_ge(sent[b], 16 * TILES // 2)
            by_tile = sorted_dram.rearrange("(s p) c -> s p c", p=P)

            def load_row(s, ahead):
                if ahead is not None or s >= 8:
                    sp.wait_ge(y_sent[s % 4], plus((s - 8) // 4 * 16 + 16, ahead, 4))
                    pass_wait(sp)
                src = by_tile[s] if ahead is None else by_tile[bass.ds(ahead + s, 1), :, :].rearrange("a p c -> (a p) c")
                sp.dma_start(ring[:, s % 8, :], src).then_inc(row_loaded[s % 8], 16)

            over_sorted(sp, load_row)

            for r in range(4):
                sp.wait_ge(y_sent[r], 16 * SORTED // 4)

        @block.gpsimd
        def _(pool):
            own = Count(pool, pool_own)
            nc.gpsimd.memset(send[:, :, :, D:ROW], 0.0)
            nc.gpsimd.memset(blank[:, 0:D], 0.0)
            nc.gpsimd.memset(blank[:, D:ROW].bitcast(I32), TOKENS).then_inc(blank_made, 1)
            own.link(nc.gpsimd.memset(neg_half[:, :], -0.5))
            for c in range(PAIRS):
                t = slice(c * PT, c * PT + PT)
                pool.wait_ge(moments_done, c + 1)
                if c >= 1:
                    pool.wait_ge(rstd_done, c)
                own.link(nc.gpsimd.tensor_scalar(var_eps[:, :], moments[:, c % 4, :, 1], 1.0, EPS, ALU.mult, ALU.add))
                nc.gpsimd.tensor_copy(mean[:, t], moments[:, c % 4, :, 0])
                nc.gpsimd.tensor_tensor(rstd[:, t], var_eps[:, :], neg_half[:, :], ALU.pow).then_inc(rstd_done, 1)

            for b in range(2):
                own.link(nc.gpsimd.memset(v_sb[b][:, :, :, :, :], 0.0))
                nc.gpsimd.memset(v_sb[b][:, :, :, :, DH:DH + 1], 1.0).then_inc(v_zeroed, 1)
            for g in range(2):
                nc.gpsimd.tensor_copy(send[:, g, :, 0:D], x_res[:, g * PT:g * PT + PT, :]).then_inc(send_made, 1)
            plain = Step()

            def split(i):
                for k, full in enumerate((q32, k32)):
                    shared_wait_used(pool, [("qk"[k], i, 0)], plain)
                    own.link(nc.gpsimd.tensor_tensor(full[:, :], full[:, :], parts[:, 3 * k, :], ALU.subtract))
                    own.link(nc.gpsimd.tensor_scalar(parts[:, 3 * k + 1, :], full[:, :], 1.0, 0.0, ALU.mult, ALU.add))
                    nc.gpsimd.tensor_tensor(parts[:, 3 * k + 2, :], full[:, :], parts[:, 3 * k + 1, :], ALU.subtract).then_inc(parts_made, 1)

            def scatter(g):
                b = g % 2
                if g == 0:
                    pool.wait_ge(blanks_stored, 16 * (SORTED // 8))
                    pool.wait_ge(routed, 1)
                    pool.wait_ge(send_made, 2)
                if g >= 2:
                    pool.wait_ge(sent[b], 16 * PT * (g // 2))
                for k in range(PT):
                    t = g * PT + k
                    nc.gpsimd.tensor_scalar(send[:, b, k, 0:D], x_res[:, t, :] if g >= 2 else send[:, b, k, 0:D],
                                            send_scale[:, t:t + 1], send_shift[:, t:t + 1], ALU.mult, ALU.add)
                made = nc.gpsimd.tensor_copy(send[:, b, :, D:D + 1].bitcast(I32),
                                             tok_sb[:, g * PT:g * PT + PT].unsqueeze(2))
                if g >= 2:
                    made.then_inc(send_made, 1)
                    pool.wait_ge(send_made, g + 1)
                else:
                    own.link(made)
                for k in range(PT):
                    t = g * PT + k
                    nc.gpsimd.indirect_dma_start(
                        sorted_dram, bass.IndirectOffsetOnAxis(slot[:, t:t + 1].bitcast(U32), 0),
                        send[:, b, k, :], None, bounds_check=SORTED * P - 1, oob_is_err=False).then_inc(sent[b], 16)

            def add_bo(i):
                shared_wait_used(pool, [("sum", 2 * i, 0), ("sum", 2 * i + 1, 0)], plain)
                t = slice(i * PT, i * PT + PT)
                nc.gpsimd.tensor_tensor(x_res[:, t, :], x_res[:, t, :], bo_sb[:, :].unsqueeze(1).to_broadcast([P, PT, D]),
                                        ALU.add).then_inc(bo_added, 1)

            def load_expert(e):
                pool.dma_start(gu_sb[:, e * 2 * F:(e + 1) * 2 * F], wgu[e]).then_inc(experts_loaded, 16)
                pool.dma_start(dn_sb[:, e * 2 * D:(e + 1) * 2 * D].rearrange("p (u d) -> p u d", u=2),
                               wdn[e].rearrange("(u p) d -> p u d", p=P)).then_inc(experts_loaded, 16)

            split(1)
            next_expert = 0
            for i in range(PAIRS):
                if i == 2:
                    split(i + 2)
                if i >= 2:
                    scatter(i)
                if i >= 1:
                    add_bo(i - 1)
                if i + 2 < PAIRS and i != 2:
                    split(i + 2)
                if i == 1:
                    scatter(0)
                    scatter(1)
                while next_expert < min(EXPERTS, 2 * (i - 1)):
                    load_expert(next_expert)
                    next_expert += 1
            add_bo(PAIRS - 1)
            pool.wait_ge(bo_added, PAIRS)
            pool.dma_start(out_by_chunk[PAIRS - 1], x_res[:, TILES - PT:TILES, :]).then_inc(last_stored, 16)
            pool.wait_ge(out_stored, 16 * (PAIRS - 1))
            pool.wait_ge(last_stored, 16)

            def send_back(s, ahead):
                pool.wait_ge(y_done, plus(s + 1, ahead))
                pass_wait(pool)
                nc.gpsimd.indirect_dma_start(
                    out, bass.IndirectOffsetOnAxis(ring[:, s % 8, D:D + 1].bitcast(U32), 0),
                    e_y[:, s % 4, :], None, bounds_check=TOKENS - 1, oob_is_err=False,
                    compute_op=ALU.add).then_inc(y_sent[s % 4], 16)

            over_sorted(pool, send_back)

        @block.scalar
        def _(act):
            act.dma_start(cst_sb[:, :], cst).then_inc(const_loaded, 16)
            act.dma_start(wr_sb[:, :], wr).then_inc(const_loaded, 16)
            act.dma_start(mask_q_sb[:, :].bitcast(U16), mask_q).then_inc(masks_loaded, 16)
            act.dma_start(mask_k_sb[:, :].bitcast(U16), mask_k).then_inc(masks_loaded, 16)
            loads = [(wq_sb[:, :], wq), (wk_sb[:, :], wk), (wv_sb[:, :], wv), (wo_sb[:, :], wo), (wg_sb[:, :], wg),
                     (wu_sb[:, :], wu), (wd_sb[:, :].rearrange("p (u d) -> p u d", u=2), wd.rearrange("(u p) d -> p u d", p=P)),
                     (bq_sb[:, :], bq), (bk_sb[:, :], bk), (bv_sb[:, :], bv.to_broadcast([P, D])),
                     (bo_sb[:, :], bo.to_broadcast([P, D])), (tok_sb[:, :], tok)]
            for dst, src in loads:
                act.dma_start(dst, src).then_inc(weights_loaded, 16)

            def take_xnT(c, b, half, runtime):
                act.wait_ge(xn_turned, c + 1)
                if runtime:
                    act.wait_ge(logits_out, c - 1)
                    act.wait_ge(xnT_stored[b], half * 16)
                act.activation(chunkT[b], first_bank[b][:, :], ACT.Copy).then_inc(xnT_done, 1)
                act.wait_ge(xnT_done, c + 1)
                dst = xnT_dram[bass.ds(c, 1), :, :].rearrange("a p n -> (a p) n") if runtime else xnT_dram[c]
                act.dma_start(dst, chunkT[b]).then_inc(xnT_stored[b], 16)

            def take_logits(c, b, runtime):
                act.wait_ge(logits_out, c + 1)
                dst = logits[:, bass.ds(c * PT, PT), :] if runtime else logits[:, c * PT:c * PT + PT, :]
                act.activation(dst, second_bank[b][:, 0:PT * E].rearrange("p (t e) -> p t e", e=E), ACT.Copy).then_inc(logits_done, 1)

            take_xnT(0, 0, 0, False)
            take_xnT(1, 1, 0, False)
            take_logits(0, 0, False)

            def two_chunks(k):
                take_xnT(k * 2, 0, k, True)
                take_logits(k * 2 - 1, 1, True)
                take_xnT(k * 2 + 1, 1, k, True)
                take_logits(k * 2, 0, True)

            with act.Fori(1, NORM_BEFORE // 2) as k:
                two_chunks(k)

            def take_qk(what, i, step):
                b = shared_wait_out(act, [(what, i, 0)], step)
                if what == "q":
                    step.wait(act, parts_made, 2 * i, 2)
                    if i >= 1:
                        step.wait(act, stack_loaded[(i - 1) % 2], 96 * ((i - 1) // 2 + 1), 48)
                full, part, scale, bias = (q32, 0, DH**-0.5, bqs) if what == "q" else (k32, 3, 1.0, bk_sb)
                act.activation(parts[:, part, :], shared_bank[b][:, :], ACT.Identity, bias=bias[:, :], scale=scale)
                act.activation(full[:, :], shared_bank[b][:, :], ACT.Identity, bias=bias[:, :], scale=scale).then_inc(shared_used[b], 1)

            def take_max(n, step):
                b = shared_wait_out(act, [("max", n, 0)], step)
                step.wait(act, max_loaded, 16 * n, 32)
                act.activation(maxT[:, :], shared_bank[b][0:3 * HEADS, 0:SEQ // 2].bitcast(BF16), ACT.Copy).then_inc(shared_used[b], 1)

            def take_att(n, step):
                step.wait(act, att_added, ITEMS * (n + 1), 2 * ITEMS)
                wait_last(act, shared_out, [("turn", n - 1, 0)], step)
                act.activation(att[:, :, :].rearrange("p s n -> p (s n)"), att_bank[n % 2][:, :],
                               ACT.Copy).then_inc(att_taken, 1)

            def take_back(n, step):
                b = shared_wait_out(act, [("back", n, 0), ("sum", n - 1, 0)], step)
                act.activation(att_nT[:, :, :].rearrange("p q n -> p (q n)"), shared_bank[b][:, 0:SEQ], ACT.Copy).then_inc(shared_used[b], 1)

            def take_gate(i, f, step):
                b = shared_wait_out(act, [("gate", i, f)], step)
                shared_wait_used(act, [("gate", i + f - 1, 1 - f)], step)
                act.activation(th[:, :], shared_bank[b][:, :], ACT.Tanh, scale=0.5).then_inc(tanh_done, 1)

            def batch(n, i, step):
                for j in range(ITEMS):
                    width = K_ITEM[j % 2][2]
                    step.wait(act, second_out, ITEMS * n + j + 1, 2 * ITEMS)
                    step.wait(act, att_added, ITEMS * n + j - 3, 2 * ITEMS)
                    act.activation(probs[:, j % 4, :, 0:width],
                                   second_bank[j % 2][:, :].rearrange("p (u w) -> p u w", u=2)[:, :, 0:width],
                                   ACT.Exp).then_inc(exp_done, 1)
                    if j == 1 and n >= 1:
                        take_att(n - 1, step)
                    if j == 6 and n >= 1:
                        take_back(n - 1, step)
                    if j == 10 and n + 1 < BATCHES:
                        take_max(n + 1, step)
                    if n % 2 == 1 and i + 1 < PAIRS and j in (0, 11):
                        take_gate(i + 1, (0, 11).index(j), step)
                    if n % 2 == 0 and i + 2 < PAIRS and j in (12, 14):
                        take_qk("q" if j == 12 else "k", i + 2, step)
                    if (n, j) == RANK_AT:
                        act.wait_ge(top_done, 1)
                        act.activation(score[:, 0:T], top[:, 0:T], ACT.Exp, scale=-1.0).then_inc(exp_top_done, 1)
                    if n < 2 and j % 3 == 0 and (6 * n + j // 3) < SORTED // 8:
                        part = 6 * n + j // 3
                        act.dma_start(sorted_dram[part * 8 * P:(part + 1) * 8 * P, :].rearrange("(p r) c -> p r c", p=P),
                                      blank[:, :].unsqueeze(1).to_broadcast([P, 8, ROW])).then_inc(blanks_stored, 16)

            plain = Step()
            take_qk("q", 0, plain)
            take_qk("k", 0, plain)
            for k in range(NORM_BEFORE // 2, PAIRS // 2):
                two_chunks(k)
            take_logits(PAIRS - 1, 1, False)
            take_qk("q", 1, plain)
            take_qk("k", 1, plain)
            take_gate(0, 0, plain)
            take_gate(0, 1, plain)
            take_max(0, plain)
            act.wait_ge(blank_made, 1)

            def pair(i, step):
                batch(2 * i, i, step)
                batch(2 * i + 1, i, step)

            over_pairs(act, pair)
            take_att(BATCHES - 1, plain)
            take_back(BATCHES - 1, plain)

            def expert_tile(s, ahead):
                def take_row(s):
                    wait_count(act, row_turned, s + 1, ahead)
                    wait_count(act, gu_out, s - 1, ahead)
                    act.activation(rowT[:, s % 2, :], second_bank[s % 2][:, 0:P], ACT.Copy).then_inc(rowT_done, 1)

                if s == 0 and ahead is None:
                    take_row(0)
                if s + 1 < SORTED or ahead is not None:
                    take_row(s + 1)
                wait_count(act, gu_out, s + 1, ahead)
                wait_count(act, e_gated_done, s - 1, ahead)
                act.activation(e_th[:, s % 2, :], first_bank[s % 2][:, 0:F], ACT.Tanh, scale=0.5).then_inc(e_tanh_done, 1)

                def take_h(s):
                    wait_count(act, h_turned, s + 1, ahead)
                    wait_count(act, y_out, s - 1, ahead)
                    act.activation(e_hT[:, s % 2, :], att_bank[s % 2][:, 0:F], ACT.Copy, scale=0.5).then_inc(e_hT_done, 1)

                if s >= 1:
                    take_h(s - 1)
                if s == SORTED - 1:
                    take_h(s)

            over_sorted(act, expert_tile)

        @block.tensor
        def _(pe):
            pe.wait_ge(const_loaded, 32)

            def turn_chunk(c, b, runtime):
                pe.wait_ge(xn_done, c + 1)
                if runtime:
                    pe.wait_ge(xnT_done, c - 1)
                for k in range(PT):
                    last = nc.tensor.transpose(first_bank[b][:, k * P:(k + 1) * P], xn[b][:, k, :], ident)
                last.then_inc(xn_turned, 1)

            def route_chunk(c, b, runtime):
                pe.wait_ge(xnT_done, c + 1)
                if runtime:
                    pe.wait_ge(logits_done, c - 1)
                for k in range(PT):
                    last = nc.tensor.matmul(second_bank[b][:, k * E:(k + 1) * E], chunkT[b][:, k * P:(k + 1) * P],
                                            wr_sb[:, :], start=True, stop=True)
                last.then_inc(logits_out, 1)

            turn_chunk(0, 0, False)
            turn_chunk(1, 1, False)
            route_chunk(0, 0, False)

            def two_chunks(k, first=False):
                turn_chunk(k * 2, 0, True)
                route_chunk(k * 2 - 1, 1, not first)
                turn_chunk(k * 2 + 1, 1, True)
                route_chunk(k * 2, 0, True)

            two_chunks(1, first=True)
            with pe.Fori(2, NORM_BEFORE // 2) as k:
                two_chunks(k)

            def project(what, i, step):
                b = shared_open(pe, (what, i, 0), step)
                step.wait(pe, xnT_loaded[i % 2], 16 * (i // 2 + 1), 8)
                nc.tensor.matmul(shared_bank[b][:, :], (wq_sb if what == "q" else wk_sb)[:, :], xnT[i % 2][:, :],
                                 start=True, stop=True).then_inc(shared_out[b], 1)

            def project_v(i, half, step):
                b = shared_open(pe, ("v", i, half), step)
                for k in (2 * half, 2 * half + 1):
                    last = nc.tensor.matmul(shared_bank[b][:, (k % 2) * D:(k % 2 + 1) * D], xnT[i % 2][:, k * P:(k + 1) * P],
                                            wv_sb[:, :], start=True, stop=True)
                last.then_inc(shared_out[b], 1)

            def gate_up(what, i, f, step):
                b = shared_open(pe, (what, i, f), step)
                w = wg_sb if what == "gate" else wu_sb
                nc.tensor.matmul(shared_bank[b][:, :], w[:, f * P:(f + 1) * P], xnT[i % 2][:, :],
                                 start=True, stop=True).then_inc(shared_out[b], 1)

            def first_scores(n, j, step):
                (q0, k0, width), i = Q_ITEM[j % 2], n // 2
                if j == 0 and n % 2 == 0:
                    step.wait(pe, stack_loaded[i % 2], 96 * (i // 2 + 1), 48)
                step.wait(pe, max_taken, ITEMS * n + j - 1, 2 * ITEMS)
                at = (n % 2) * SEQ
                for u in range(2):
                    h = 2 * (j // 2) + u
                    last = nc.tensor.matmul(first_bank[j % 2][:, u * 256:u * 256 + width],
                                            stack[i % 2][0:ROWS_Q, h, 0, at + q0:at + q0 + P],
                                            stack[i % 2][0:ROWS_Q, h, 1, at + k0:at + k0 + width], start=True, stop=True)
                last.then_inc(first_out, 1)

            def second_scores(n, j, step):
                (k0, q0, width), i = K_ITEM[j % 2], n // 2
                if j == 0:
                    step.wait(pe, max_loaded, 16 * (n + 1), 32)
                step.wait(pe, exp_done, ITEMS * n + j - 1, 2 * ITEMS)
                at = (n % 2) * SEQ
                for u in range(2):
                    h = 2 * (j // 2) + u
                    last = nc.tensor.matmul(second_bank[j % 2][:, u * 256:u * 256 + width],
                                            stack[i % 2][0:ROWS_K, h, 1, at + k0:at + k0 + P],
                                            stack[i % 2][0:ROWS_K, h, 0, at + q0:at + q0 + width], start=True, stop=True)
                last.then_inc(second_out, 1)

            def add_values(n, j, step):
                (_, q0, width), i = K_ITEM[j % 2], n // 2
                step.wait(pe, exp_done, ITEMS * n + j + 1, 2 * ITEMS)
                if j == 0:
                    if n % 2 == 0:
                        shared_wait_used(pe, [("v", i, 0), ("v", i, 1)], step)
                    step.wait(pe, att_taken, n - 1, 2)
                for u in range(2):
                    h = 2 * (j // 2) + u
                    group, place = h % GROUPS, h // GROUPS
                    row, col = 32 * (group % 4), SEQ * (group // 4) + q0
                    values = v_sb[i % 2][:, 2 * (n % 2) + j % 2, group, :, :].rearrange("p s e -> p (s e)")
                    last = nc.tensor.matmul(att_bank[n % 2][row:row + 2 * (DH + 1), col:col + width],
                                            values[:, place * (DH + 1):(place + 2) * (DH + 1)], probs[:, j % 4, u, 0:width],
                                            start=(h < 4 and j % 2 == 0), stop=(j % 2 == 1), skip_group_check=True)
                last.then_inc(att_added, 1)

            def turn(n, step):
                b = shared_open(pe, ("turn", n, 0), step)
                step.wait(pe, att_taken, n + 1, 2)
                for qt in range(2):
                    for s in range(2):
                        last = nc.tensor.transpose(shared_bank[b][:, (2 * qt + s) * P:(2 * qt + s + 1) * P],
                                                   att[:, s, qt * P:(qt + 1) * P], ident)
                last.then_inc(shared_out[b], 1)

            def back(n, step):
                b = shared_open(pe, ("back", n, 0), step, after=[("turn", n, 0)])
                for qt in range(2):
                    last = nc.tensor.transpose(shared_bank[b][:, qt * P:(qt + 1) * P], att_n[:, qt, :], ident)
                last.then_inc(shared_out[b], 1)

            def sum_rest(n, step):
                i = n // 2
                b = shared_open(pe, ("sum", n, 0), step, after=[("back", n, 0), ("up", i, 0), ("up", i, 1)])
                for qt in range(2):
                    into = shared_bank[b][:, qt * D:(qt + 1) * D]
                    nc.tensor.matmul(into, att_nT[:, qt, :], wo_sb[:, :], start=True, stop=False)
                    at = (n % 2) * SEQ + qt * P
                    for f in range(2):
                        last = nc.tensor.matmul(into, hT[:, i % 2, f, at:at + P], wd_sb[:, f * D:(f + 1) * D],
                                                start=False, stop=(f == 1))
                last.then_inc(shared_out[b], 1)

            def turn_max(n, step):
                step.wait(pe, max_split, n + 1, 2)
                b = shared_open(pe, ("max", n, 0), step)
                pass_wait(pe)
                view = shared_bank[b][:, :].bitcast(BF16)
                for qt in range(2):
                    last = nc.tensor.transpose(view[0:3 * HEADS, qt * P:(qt + 1) * P],
                                               max_parts[:, qt, :, :].rearrange("p a h -> p (a h)"), ident_bf[:, :])
                last.then_inc(shared_out[b], 1)

            def rank(step):
                b = shared_open(pe, ("rank", 0, 0), step)
                pe.wait_ge(counted, 1)
                nc.tensor.matmul(shared_bank[b][:, 0:E], before, row_count[:, 0:E], start=True, stop=True)
                nc.tensor.matmul(shared_bank[b][:, E:2 * E], ones[:, :], row_count[:, 0:E], start=True, stop=True).then_inc(shared_out[b], 1)

            def shared_use(what, of, part, step):
                if what in ("q", "k"):
                    project(what, of, step)
                elif what == "rank":
                    rank(step)
                elif what == "v":
                    project_v(of, part, step)
                elif what in ("gate", "up"):
                    gate_up(what, of, part, step)
                else:
                    {"turn": turn, "back": back, "sum": sum_rest, "max": turn_max}[what](of, step)

            plain = Step()
            pe.wait_ge(weights_loaded, 16 * 12)
            pe.wait_ge(prepared, 1)
            project("q", 0, plain)
            project("k", 0, plain)
            for k in range(NORM_BEFORE // 2, PAIRS // 2):
                two_chunks(k)
            route_chunk(PAIRS - 1, 1, True)
            project("q", 1, plain)
            project("k", 1, plain)
            for j in range(ITEMS):
                first_scores(0, j, plain)
                if j % 2 == 1 and j // 2 < len(FIRST_USES):
                    shared_use(*FIRST_USES[j // 2], plain)
            turn_max(0, plain)
            for j in range(LEAD):
                first_scores(1, j, plain)

            def batch(n, i, step):
                for j in range(ITEMS):
                    ahead_n, ahead_j = n + 1 + (j + LEAD) // ITEMS, (j + LEAD) % ITEMS
                    if ahead_n < BATCHES:
                        first_scores(ahead_n, ahead_j, step)
                    second_scores(n, j, step)
                    if j >= 2:
                        add_values(n, j - 2, step)
                    elif n >= 1:
                        add_values(n - 1, ITEMS - 2 + j, step)
                    for use in shared_uses_after(n, j):
                        shared_use(*use, step)

            def pair(i, step):
                batch(2 * i, i, step)
                batch(2 * i + 1, i, step)

            over_pairs(pe, pair)
            add_values(BATCHES - 1, ITEMS - 2, plain)
            add_values(BATCHES - 1, ITEMS - 1, plain)
            for what in ("turn", "back", "sum"):
                shared_use(what, BATCHES - 1, 0, plain)

            pe.wait_ge(experts_loaded, 32)

            experts = {}

            def expert_tile(s, ahead):
                def load_expert_of(s):
                    at = expert_of[0:1, s + 2:s + 3] if ahead is None else expert_of[0:1, bass.ds(ahead + s + 2, 1)]
                    _, got = nc.values_load_multi_w_load_instructions(at, engines=[pe.engine], min_val=0, max_val=EXPERTS - 1)
                    experts[s] = got[0]

                if s % 8 == 0:
                    load_expert_of(s)

                def turn_row(s):
                    if ahead is None:
                        pe.wait_ge(row_loaded[s % 8], 16 * (s // 8 + 1))
                    else:
                        pe.wait_ge(row_loaded[s % 8], ahead * 2 + 16 * (s // 8 + 1))
                    wait_count(pe, rowT_done, s - 1, ahead)
                    nc.tensor.transpose(second_bank[s % 2][:, 0:P], ring[:, s % 8, 0:D], ident).then_inc(row_turned, 1)

                def turn_h(s):
                    wait_count(pe, h_done, s + 1, ahead)
                    wait_count(pe, e_hT_done, s - 1, ahead)
                    for f in range(2):
                        last = nc.tensor.transpose(att_bank[s % 2][:, f * P:(f + 1) * P], e_h[:, s % 2, f * P:(f + 1) * P], ident)
                    last.then_inc(h_turned, 1)

                def down(s):
                    wait_count(pe, e_hT_done, s + 1, ahead)
                    wait_count(pe, y_done, s - 1, ahead)
                    for f in range(2):
                        last = nc.tensor.matmul(shared_bank[s % 2][:, 0:D], e_hT[:, s % 2, f * P:(f + 1) * P],
                                                dn_sb[:, bass.ds(experts[s] * (2 * D) + f * D, D)], start=(f == 0), stop=(f == 1))
                    last.then_inc(y_out, 1)

                if s == 0 and ahead is None:
                    turn_row(0)
                if s + 1 < SORTED:
                    turn_row(s + 1)
                wait_count(pe, rowT_done, s + 1, ahead)
                wait_count(pe, h_done, s - 1, ahead)
                nc.tensor.matmul(first_bank[s % 2][:, :], rowT[:, s % 2, :], gu_sb[:, bass.ds(experts[s] * (2 * F), 2 * F)],
                                 start=True, stop=True).then_inc(gu_out, 1)
                if s % 8 < 2 and s >= 8:
                    load_expert_of(s - 2)
                if s % 8 < 7:
                    load_expert_of(s + 1)
                if s >= 1:
                    turn_h(s - 1)
                if s >= 2:
                    down(s - 2)
                if s == SORTED - 1:
                    turn_h(s)
                    down(s - 1)
                    down(s)

            over_sorted(pe, expert_tile)

        @block.vector
        def _(dve):
            own = Count(dve, dve_own)
            nc.vector.memset(ones[:, :], 1.0)
            for b in range(2):
                nc.vector.memset(att_bank[b][:, :], 0.0)
            nc.vector.memset(expert_of[:, :], 0)

            def take_stats(c, loads, b, ring4, runtime):
                dve.wait_ge(x_loaded[ring4], loads * 16)
                for k in range(PT):
                    src = x_res[:, bass.ds(c * PT + k, 1), :] if runtime else x_res[:, c * PT + k:c * PT + k + 1, :]
                    last = nc.vector.bn_stats(stats[:, b, k, :], src.rearrange("p a d -> p (a d)"))
                last.then_inc(stats_done, 1)
                dve.wait_ge(stats_done, c + 1)
                pass_wait(dve)
                for k in range(PT):
                    last = nc.vector.bn_aggr(moments[:, ring4, k, :], stats[:, b, k, :])
                last.then_inc(moments_done, 1)

            def norm(c, b, ring4, runtime):
                dve.wait_ge(rstd_done, c + 1)
                if runtime or c >= 2:
                    dve.wait_ge(xn_turned, c - 1)
                for k in range(PT):
                    t = c * PT + k
                    src = x_res[:, bass.ds(t, 1), :].rearrange("p a d -> p (a d)") if runtime else x_res[:, t, :]
                    r = rstd[:, bass.ds(t, 1)] if runtime else rstd[:, t:t + 1]
                    last = nc.vector.tensor_scalar(xn[b][:, k, :], src, moments[:, ring4, k, 0:1], r, ALU.subtract, ALU.mult)
                last.then_inc(xn_done, 1)

            for c in range(4):
                take_stats(c, 1, c % 2, c % 4, False)
                if c >= 1:
                    norm(c - 1, (c - 1) % 2, (c - 1) % 4, False)
            dve.wait_ge(weights_loaded, 16 * 12)
            nc.vector.tensor_scalar(bqs[:, :], bq_sb[:, :], DH**-0.5, None, ALU.mult)
            nc.vector.tensor_copy(ident_bf[:, :], ident).then_inc(prepared, 1)
            with dve.Fori(0, NORM_BEFORE // 4 - 1) as turn:
                for c in range(4, 8):
                    take_stats(turn * 4 + c, turn + 2, c % 2, c % 4, True)
                    norm(turn * 4 + (c - 1), (c - 1) % 2, (c - 1) % 4, True)

            plain = Step()

            def split_first():
                for k, full in enumerate((q32, k32)):
                    shared_wait_used(dve, [("qk"[k], 0, 0)], plain)
                    own.link(nc.vector.tensor_tensor(full[:, :], full[:, :], parts[:, 3 * k, :], ALU.subtract))
                    own.link(nc.vector.tensor_copy(parts[:, 3 * k + 1, :], full[:, :]))
                    nc.vector.tensor_tensor(parts[:, 3 * k + 2, :], full[:, :], parts[:, 3 * k + 1, :], ALU.subtract).then_inc(parts_made, 1)

            for c in range(NORM_BEFORE, PAIRS):
                take_stats(c, c // 4 + 1, c % 2, c % 4, False)
                norm(c - 1, (c - 1) % 2, (c - 1) % 4, False)
                if c == NORM_BEFORE + 2:
                    split_first()
            norm(PAIRS - 1, 1, 3, False)

            def take_v(i, half, step):
                b = shared_wait_out(dve, [("v", i, half)], step)
                if i + half == 0:
                    dve.wait_ge(v_zeroed, 2)
                by_place = "p (s g d) -> p g s d"
                for k in range(2):
                    last = nc.vector.tensor_tensor(v_sb[i % 2][:, 2 * half + k, :, :, 0:DH],
                                                   shared_bank[b][:, k * D:(k + 1) * D].rearrange(by_place, s=2, d=DH),
                                                   bv_sb[:, :].rearrange(by_place, s=2, d=DH), ALU.add)
                last.then_inc(shared_used[b], 1)

            def over_experts(ap):
                return ap.unsqueeze(2).to_broadcast([P, T, E])

            def over_tiles(ap):
                return ap.unsqueeze(1).to_broadcast([P, T, E])

            tallies = [hot, tally_a, tally_b, tally_a, tally_b, tally_a, tally_b]
            tally = tallies[-1]
            exceeds = marks.rearrange("p t e -> p (t e)").rearrange("p (e t) -> p e t", e=E)
            which = slot_f

            def route(part):
                own.settle()
                if part == 0:
                    dve.wait_ge(logits_done, PAIRS)
                    nc.vector.tensor_copy(rev_bf[:, 0:E], rev)
                    nc.vector.tensor_copy(tile_bf[:, 0:SORTED], tile_no)
                    nc.vector.tensor_reduce(top[:, 0:T], logits, AX.X, ALU.max).then_inc(top_done, 1)
                elif part == 1:
                    dve.wait_ge(top_done, 1)
                    own.mark(nc.vector.tensor_tensor(marks, logits, over_experts(top[:, 0:T]), ALU.is_equal))
                elif part == 2:
                    own.mark(nc.vector.tensor_tensor(marks, marks, over_tiles(rev_bf[:, 0:E]), ALU.mult))
                elif part == 3:
                    own.mark(nc.vector.tensor_reduce(first[:, 0:T], marks, AX.X, ALU.max))
                elif part == 4:
                    own.mark(nc.vector.tensor_tensor(hot, over_tiles(rev_bf[:, 0:E]), over_experts(first[:, 0:T]), ALU.is_equal))
                elif part == 5:
                    nc.vector.tensor_reduce(row_count[:, 0:E], hot.rearrange("p t e -> p e t"), AX.X, ALU.add).then_inc(counted, 1)
                elif part < 12:
                    src, dst, s = tallies[part - 6], tallies[part - 5], 1 << (part - 6)
                    nc.vector.tensor_copy(dst[:, 0:s, :], src[:, 0:s, :])
                    own.mark(nc.vector.tensor_tensor(dst[:, s:T, :], src[:, s:T, :], src[:, 0:T - s, :], ALU.add))
                elif part == 12:
                    shared_wait_used(dve, [("rank", 0, 0)], plain)
                    own.mark(nc.vector.tensor_tensor(exceeds, ranks[:, E:2 * E].unsqueeze(2).to_broadcast([P, E, T]),
                                                     steps128.unsqueeze(1).to_broadcast([P, E, T]), ALU.is_gt))
                elif part == 13:
                    own.link(nc.vector.tensor_reduce(n_tiles[:, 0:E], exceeds, AX.X, ALU.add))
                    src = n_tiles
                    for k, s in enumerate((1, 2, 4, 8)):
                        dst = (ends_a, ends)[k % 2]
                        nc.vector.tensor_copy(dst[:, 0:s], src[:, 0:s])
                        own.link(nc.vector.tensor_tensor(dst[:, s:E], src[:, s:E], src[:, 0:E - s], ALU.add))
                        src = dst
                    nc.vector.tensor_copy(ends_bf[:, 0:E], ends[:, 0:E])
                    own.link(nc.vector.tensor_tensor(base[:, 0:E], ends[:, 0:E], n_tiles[:, 0:E], ALU.subtract))
                    own.link(nc.vector.tensor_scalar(base[:, 0:E], base[:, 0:E], float(P), -1.0, ALU.mult, ALU.add))
                    own.mark(nc.vector.tensor_tensor(base[:, 0:E], ranks[:, 0:E], base[:, 0:E], ALU.add))
                elif part == 14:
                    own.mark(nc.vector.tensor_tensor(work, tally, over_tiles(base[:, 0:E]), ALU.add))
                elif part == 15:
                    own.mark(nc.vector.tensor_tensor(work, work, hot, ALU.mult))
                elif part == 16:
                    own.link(nc.vector.tensor_reduce(slot_f[:, 0:T], work, AX.X, ALU.add))
                    own.mark(nc.vector.tensor_copy(slot[:, :], slot_f[:, 0:T]))
                elif part == 17:
                    own.mark(nc.vector.tensor_tensor(compare, tile_bf[:, 0:SORTED].unsqueeze(2).to_broadcast([P, SORTED, E]),
                                                     ends_bf[:, 0:E].unsqueeze(1).to_broadcast([P, SORTED, E]), ALU.is_ge))
                elif part == 18:
                    own.link(nc.vector.tensor_reduce(which[:, 0:SORTED], compare, AX.X, ALU.add))
                    own.mark(nc.vector.tensor_scalar(expert_of[:, 2:2 + SORTED], which[:, 0:SORTED], float(E - 1), None, ALU.min))
                else:
                    dve.wait_ge(exp_top_done, 1)
                    own.link(nc.vector.tensor_scalar(score[:, 0:T], score[:, 0:T], 1.0, None, ALU.add))
                    own.link(nc.vector.reciprocal(score[:, 0:T], score[:, 0:T]))
                    own.link(nc.vector.tensor_tensor(send_scale[:, :], score[:, 0:T], rstd[:, :], ALU.mult))
                    nc.vector.scalar_tensor_tensor(send_shift[:, :], mean[:, :], -1.0, send_scale[:, :], ALU.mult, ALU.mult).then_inc(routed, 1)

            def take_ranks():
                b = shared_wait_out(dve, [("rank", 0, 0)], plain)
                nc.vector.tensor_copy(ranks[:, 0:2 * E], shared_bank[b][:, 0:2 * E]).then_inc(shared_used[b], 1)

            def take_first(n, j, step):
                width = Q_ITEM[j % 2][2]
                step.wait(dve, first_out, ITEMS * n + j + 1, 2 * ITEMS)
                if j == 0:
                    step.wait(dve, max_split, n - 1, 2)
                nc.vector.tensor_reduce(neg_max[:, n % 2, j % 2, 2 * (j // 2):2 * (j // 2) + 2],
                                        first_bank[j % 2][:, :].rearrange("p (u w) -> p u w", u=2)[:, :, 0:width],
                                        AX.X, ALU.max, negate=True).then_inc(max_taken, 1)

            def split_max(n, step):
                step.wait(dve, max_taken, ITEMS * (n + 1), 2 * ITEMS)
                wait_last(dve, shared_out, [("max", n - 1, 0)], step)
                full = neg_max[:, n % 2, :, :]
                own.link(nc.vector.tensor_copy(max_parts[:, :, 0, :], full))
                own.link(nc.vector.tensor_tensor(full, full, max_parts[:, :, 0, :], ALU.subtract))
                own.link(nc.vector.tensor_copy(max_parts[:, :, 1, :], full))
                nc.vector.tensor_tensor(max_parts[:, :, 2, :], full, max_parts[:, :, 1, :],
                                        ALU.subtract).then_inc(max_split, 1)

            def normalise(n, step):
                b = shared_wait_out(dve, [("turn", n, 0), ("back", n - 1, 0)], step)
                heads = shared_bank[b][:, :].rearrange("p (g r) -> p g r", r=32)[:, :, 0:2 * (DH + 1)]
                heads = heads.rearrange("p g (s e) -> p g s e", s=2)
                nc.vector.reciprocal(recip[:, :, :], heads[:, :, :, DH]).then_inc(recip_done, 1)
                step.wait(dve, recip_done, n + 1, 2)
                nc.vector.tensor_tensor(att_n[:, :, :].rearrange("p q (g s d) -> p (q g) s d", s=2, d=DH), heads[:, :, :, 0:DH],
                                        recip[:, :, :].unsqueeze(3).to_broadcast([P, 2 * GROUPS, 2, DH]), ALU.mult).then_inc(shared_used[b], 1)

            def add_rest(n, step):
                b = shared_wait_out(dve, [("sum", n, 0)], step)
                if n % 2 == 0:
                    step.wait(dve, send_made, n // 2 + 1, 1)
                at = x_res[:, 2 * n:2 * n + 2, :] if step.ahead is None else x_res[:, bass.ds(step.ahead * PT + 2 * n, 2), :]
                nc.vector.tensor_tensor(at, shared_bank[b][:, 0:2 * D].rearrange("p (q d) -> p q d", q=2), at, ALU.add).then_inc(shared_used[b], 1)

            def take_gate(i, f, step):
                b = shared_wait_out(dve, [("gate", i, f)], step)
                step.wait(dve, tanh_done, 2 * i + f + 1, 2)
                shared_wait_used(dve, [("up", i + f - 1, 1 - f)], step)
                nc.vector.scalar_tensor_tensor(gated[:, :], th[:, :], 1.0, shared_bank[b][:, :], ALU.add, ALU.mult).then_inc(shared_used[b], 1)

            def take_up(i, f, step):
                shared_wait_used(dve, [("gate", i, f)], step)
                b = shared_wait_out(dve, [("up", i, f), ("sum", 2 * i - 3, 0)], step)
                nc.vector.scalar_tensor_tensor(hT[:, i % 2, f, :], gated[:, :], 0.5, shared_bank[b][:, :], ALU.mult, ALU.mult).then_inc(shared_used[b], 1)

            def batch(n, i, step):
                for j in range(ITEMS):
                    ahead_n, ahead_j = n + 1 + (j + LEAD) // ITEMS, (j + LEAD) % ITEMS
                    if ahead_n < BATCHES:
                        take_first(ahead_n, ahead_j, step)
                        if ahead_j == ITEMS - 1:
                            split_max(ahead_n, step)
                    if n >= 1 and j == 4:
                        normalise(n - 1, step)
                    if n >= 1 and j == 10:
                        add_rest(n - 1, step)
                    if n % 2 == 1 and i + 1 < PAIRS:
                        if j in (1, 12):
                            take_gate(i + 1, (1, 12).index(j), step)
                        if j in (2, 14):
                            take_up(i + 1, (2, 14).index(j), step)
                    if n % 2 == 0 and i + 1 < PAIRS and j in (2, 6):
                        take_v(i + 1, (2, 6).index(j), step)
                    if (n, j) == (RANK_AT[0] + 1, 0):
                        take_ranks()
                    if (n, j) in ROUTE_AT:
                        route(ROUTE_AT.index((n, j)))

            for j in range(ITEMS):
                take_first(0, j, plain)
                if j % 2 == 0 and 1 <= j // 2 <= len(FIRST_USES):
                    what, _, part = FIRST_USES[j // 2 - 1]
                    {"v": take_v, "gate": take_gate, "up": take_up}[what](0, part, plain)
            split_max(0, plain)
            for j in range(LEAD):
                take_first(1, j, plain)

            def pair(i, step):
                batch(2 * i, i, step)
                batch(2 * i + 1, i, step)

            over_pairs(dve, pair, own, 4 * 3)
            normalise(BATCHES - 1, plain)
            add_rest(BATCHES - 1, plain)

            def expert_tile(s, ahead):
                wait_count(dve, e_tanh_done, s + 1, ahead)
                wait_count(dve, h_done, s - 1, ahead)
                nc.vector.scalar_tensor_tensor(e_gated[:, s % 2, :], e_th[:, s % 2, :], 1.0, first_bank[s % 2][:, 0:F], ALU.add, ALU.mult).then_inc(e_gated_done, 1)
                wait_count(dve, e_gated_done, s + 1, ahead)
                wait_count(dve, h_turned, s - 1, ahead)
                nc.vector.tensor_tensor(e_h[:, s % 2, :], first_bank[s % 2][:, F:2 * F], e_gated[:, s % 2, :], ALU.mult).then_inc(h_done, 1)

                def take_y(s):
                    wait_count(dve, y_out, s + 1, ahead)
                    if ahead is not None or s >= 4:
                        dve.wait_ge(y_sent[s % 4], plus(s // 4 * 16, ahead, 4))
                    nc.vector.tensor_copy(e_y[:, s % 4, :], shared_bank[s % 2][:, 0:D]).then_inc(y_done, 1)

                if s >= 2:
                    take_y(s - 2)
                if s == SORTED - 1:
                    take_y(s - 1)
                    take_y(s)

            over_sorted(dve, expert_tile)


def constants():
    p = np.arange(P)
    rev = np.broadcast_to(EXPERTS - np.arange(EXPERTS), (P, EXPERTS))
    steps128 = np.broadcast_to(P * np.arange(TILES), (P, TILES))
    tile_no = np.broadcast_to(np.arange(SORTED), (P, SORTED))
    cst = np.concatenate([np.eye(P), p[:, None] < p[None, :], rev, steps128, tile_no], 1).astype(np.float32)
    mask_q, mask_k = np.zeros((P, PAIR), np.float32), np.zeros((P, PAIR), np.float32)
    pos = np.arange(PAIR) % SEQ
    blk, off = pos // WINDOW, pos % WINDOW
    for r, row in enumerate(FINE_ROWS):
        parity, key = r // WINDOW, r % WINDOW
        allowed = np.where(blk % 2 == parity, key <= off, key > off)
        mask_q[row] = np.where(allowed, 0.0, FAR)
        mask_k[row] = (blk % 2 == parity) & (off == key)
    for b, row in enumerate(BLOCK_ROWS):
        mask_q[row] = np.where((b == blk) | (b == blk - 1), 0.0, FAR)
        mask_k[row] = blk == b
    mask_k[MAX_ROW:MAX_ROW + 3] = 1.0
    tok = (np.arange(TILES)[None, :] * P + p[:, None]).astype(np.int32)
    mask_q, mask_k = ((m.view(np.uint32) >> 16).astype(np.uint16) for m in (mask_q, mask_k))
    return cst, mask_q, mask_k, tok


def kernel(**inputs):
    import concourse.bacc as _bacc
    from concourse.bass_utils import run_bass_kernel_spmd as _run

    g = {k.removeprefix("L0_"): np.asarray(v) for k, v in inputs.items()}

    def by_dim_then_head(w):
        return w.reshape(HEADS, DH, -1).swapaxes(0, 1).reshape(D, -1)

    cst, mask_q, mask_k, tok = constants()
    arrays = {
        "x": g["attn_x"].reshape(TOKENS, D),
        "wq": by_dim_then_head(g["attn_Wq"]).T, "bq": by_dim_then_head(g["attn_bq"]),
        "wk": by_dim_then_head(g["attn_Wk"]).T, "bk": by_dim_then_head(g["attn_bk"]),
        "wv": g["attn_Wv"].T, "bv": g["attn_bv"].reshape(1, D),
        "wo": g["attn_Wo"].T.reshape(2, GROUPS, DH, D).swapaxes(0, 1).reshape(D, D), "bo": g["attn_bo"].reshape(1, D),
        "wr": g["ffn_w_router"].T, "wgu": g["ffn_gate_up_proj"], "wdn": g["ffn_down_proj"],
        "wg": g["ffn_w_gate"].T, "wu": g["ffn_w_up"].T, "wd": g["ffn_w_down"].T,
        "cst": cst, "mask_q": mask_q, "mask_k": mask_k, "tok": tok,
    }
    nc = _bacc.Bacc("TRN2", target_bir_lowering=False, num_devices=1)
    args, given = [], {}
    for name, a in arrays.items():
        given[f"in_{name}"] = a = np.ascontiguousarray(a)
        args.append(nc.dram_tensor(f"in_{name}", list(a.shape), mybir.dt.from_np(a.dtype), kind="ExternalInput").ap())
    out = nc.dram_tensor("out_0", [TOKENS, D], F32, kind="ExternalOutput").ap()
    build(nc, *args, out)
    r = _run(nc, [given], core_ids=[0])
    return r.results[0]["out_0"].reshape(BATCHES, SEQ, D)
```
